# Optimizing a Trainium2 kernel written in Bass

```python
import numpy as np
import jax
import jax.numpy as jnp

def _softmax(x, axis=-1):
    return jax.nn.softmax(x, axis=axis)

def _gelu(x):
    return jax.nn.gelu(x, approximate=True)

def _silu(x):
    return jax.nn.silu(x)

def _sigmoid(x):
    return jax.nn.sigmoid(x)

def _layernorm(x, axis=-1, eps=1e-05):
    m = jnp.mean(x, axis=axis, keepdims=True)
    v = jnp.var(x, axis=axis, keepdims=True)
    return (x - m) / jnp.sqrt(v + eps)

def _scatter_add(tgt, idx, src, axis=0):
    return tgt.at[idx].add(src)

def _segment_sum(src, seg, n):
    return jax.ops.segment_sum(src, seg, n)
kernel_name = 'mk_adaln_d1_jaxref_r8_be4a76'

def setup_inputs(seed: int=0):
    np.random.seed(seed)
    _w = jnp.asarray

    def _L0_attn_setup():
        import jax, jax.numpy as jnp
        import numpy as np

        def _prefix_scan_causal(x, a):

            def combine(c1, c2):
                a1, x1 = c1
                a2, x2 = c2
                return (a2 * a1, a2 * x1 + x2)
            _, h = jax.lax.associative_scan(combine, (a, x), axis=1)
            return h
        key = jax.random.key(seed)
        ks = jax.random.split(key, 4)
        B, S, D = (8, 512, 128)
        scale = 1.0 / np.sqrt(D)
        x = jax.random.normal(ks[0], (B, S, D), dtype=jnp.float32)
        Wg = jax.random.normal(ks[1], (D, D), dtype=jnp.float32) * scale
        Wv = jax.random.normal(ks[2], (D, D), dtype=jnp.float32) * scale
        Wd = jax.random.normal(ks[3], (D, D), dtype=jnp.float32) * scale
        bg = jnp.zeros((D,), jnp.float32)
        bv = jnp.zeros((D,), jnp.float32)
        bd = jnp.full((D,), 1.0, jnp.float32)
        return {'x': x, 'Wg': Wg, 'bg': bg, 'Wv': Wv, 'bv': bv, 'Wd': Wd, 'bd': bd}
    _L0_attn_in = _L0_attn_setup()

    def _L0_ffn_setup():
        import jax, jax.numpy as jnp
        import numpy as np
        D, H, O, E, TOPK = (128, 512, 128, 8, 2)
        B, L = (2, 256)
        ROUTE_SCALE = 1.0
        key = jax.random.key(seed)
        ks = jax.random.split(key, 7)
        gb = float(np.sqrt(6.0 / (E + D)))
        return {'x': jax.random.normal(ks[0], (B, L, D), dtype=jnp.float32), 'gate_w': jax.random.uniform(ks[1], (E, D), jnp.float32, -gb, gb), 'gate_b': jnp.zeros((E,), jnp.float32), 'w1': jax.random.normal(ks[2], (E, D, H), jnp.float32) * 0.02, 'b1': jnp.zeros((E, H), jnp.float32), 'w2': jax.random.normal(ks[3], (E, H, O), jnp.float32) * 0.02, 'b2': jnp.zeros((E, O), jnp.float32)}
    _L0_ffn_in = _L0_ffn_setup()
    _L0_c = _w((lambda *s: np.random.randn(*s).astype(np.float32) * 0.05)(32, 128))
    _L0_wmod = _w((lambda *s: np.random.randn(*s).astype(np.float32) * 0.05)(128, 6 * 128) * 128 ** (-0.5))
    _d = {'L0_attn_x': _L0_attn_in['x'], 'L0_attn_Wg': _L0_attn_in['Wg'], 'L0_attn_bg': _L0_attn_in['bg'], 'L0_attn_Wv': _L0_attn_in['Wv'], 'L0_attn_bv': _L0_attn_in['bv'], 'L0_attn_Wd': _L0_attn_in['Wd'], 'L0_attn_bd': _L0_attn_in['bd'], 'L0_ffn_gate_w': _L0_ffn_in['gate_w'], 'L0_ffn_gate_b': _L0_ffn_in['gate_b'], 'L0_ffn_w1': _L0_ffn_in['w1'], 'L0_ffn_b1': _L0_ffn_in['b1'], 'L0_ffn_w2': _L0_ffn_in['w2'], 'L0_ffn_b2': _L0_ffn_in['b2'], 'L0_c': _L0_c, 'L0_wmod': _L0_wmod}
    _x0 = _d['L0_attn_x']
    _d['L0_attn_x'] = jax.random.normal(jax.random.fold_in(jax.random.key(seed), 1), (32, 256, 128), dtype=_x0.dtype)
    del _x0
    return _d

def reference(L0_attn_x, L0_attn_Wg, L0_attn_bg, L0_attn_Wv, L0_attn_bv, L0_attn_Wd, L0_attn_bd, L0_ffn_gate_w, L0_ffn_gate_b, L0_ffn_w1, L0_ffn_b1, L0_ffn_w2, L0_ffn_b2, L0_c, L0_wmod):

    def _L0_attn_ref(x, Wg, bg, Wv, bv, Wd, bd):
        import jax, jax.numpy as jnp
        import numpy as np

        def _prefix_scan_causal(x, a):

            def combine(c1, c2):
                a1, x1 = c1
                a2, x2 = c2
                return (a2 * a1, a2 * x1 + x2)
            _, h = jax.lax.associative_scan(combine, (a, x), axis=1)
            return h
        g = jax.nn.sigmoid(jnp.einsum('bsd,ed->bse', x, Wg) + bg)
        a = jax.nn.sigmoid(jnp.einsum('bsd,ed->bse', x, Wd) + bd)
        v = jnp.einsum('bsd,ed->bse', x, Wv) + bv
        h = _prefix_scan_causal((1.0 - a) * v, a)
        return h * g

    def _L0_ffn_ref(x, gate_w, gate_b, w1, b1, w2, b2):
        import jax, jax.numpy as jnp
        import numpy as np
        D, H, O, E, TOPK = (128, 512, 128, 8, 2)
        B, L = (2, 256)
        ROUTE_SCALE = 1.0
        Bb, Ll, Dd = x.shape
        N = Bb * Ll
        x_flat = x.reshape(N, Dd)
        logits = x_flat @ gate_w.T + gate_b
        probs = jax.nn.softmax(logits * ROUTE_SCALE, axis=-1)
        topk_vals, topk_idx = jax.lax.top_k(probs, TOPK)
        dense_gate = jnp.zeros((N, E), probs.dtype).at[jnp.arange(N)[:, None], topk_idx].set(topk_vals)
        h = jax.nn.relu(jnp.einsum('nd,edh->neh', x_flat, w1) + b1)
        y = jnp.einsum('neh,eho->neo', h, w2) + b2
        out_flat = jnp.einsum('ne,neo->no', dense_gate, y)
        return out_flat.reshape(Bb, Ll, O)
    x = L0_attn_x
    mod = (_silu(L0_c) @ L0_wmod).reshape(L0_c.shape[0], 6, 1, -1)
    sa, ca, ga, sb, cb, gb = (mod[:, 0], mod[:, 1], mod[:, 2], mod[:, 3], mod[:, 4], mod[:, 5])
    ga = (2 * (ga >= 0) - 1) * jnp.maximum(jnp.abs(ga), 0.25)
    gb = (2 * (gb >= 0) - 1) * jnp.maximum(jnp.abs(gb), 0.25)
    h = _layernorm(x, axis=-1) * (1 + ca) + sa
    x = x + ga * _L0_attn_ref(h, L0_attn_Wg, L0_attn_bg, L0_attn_Wv, L0_attn_bv, L0_attn_Wd, L0_attn_bd)
    h = _layernorm(x, axis=-1) * (1 + cb) + sb
    x = x + gb * _L0_ffn_ref(h, L0_ffn_gate_w, L0_ffn_gate_b, L0_ffn_w1, L0_ffn_b1, L0_ffn_w2, L0_ffn_b2)
    return x

_drawn_inputs = setup_inputs


def setup_inputs(seed=0):
    import zlib

    import numpy as np

    out = dict(_drawn_inputs(seed))
    spreads = {'L0_attn_bg': (0.0, 0.8),
     'L0_attn_bv': (0.0, 0.632),
     'L0_attn_bd': (1.0, 0.6),
     'L0_ffn_gate_b': (0.0, 0.8),
     'L0_ffn_b1': (0.0, 0.8),
     'L0_ffn_b2': (0.0, 0.612)}
    factors = {'L0_ffn_gate_w': 3.684, 'L0_ffn_w1': 6.886, 'L0_ffn_w2': 5.409}
    for name, (base, spread) in spreads.items():
        noise = np.random.default_rng([zlib.crc32(name.encode()), seed]).standard_normal(out[name].shape)
        drawn = base * np.exp(spread * noise) if base else spread * noise
        out[name] = jnp.asarray(drawn.astype(out[name].dtype))
    for name, factor in factors.items():
        out[name] = (out[name] * factor).astype(out[name].dtype)
    return out
```

```python
from contextlib import ExitStack

import concourse.bass as bass
from concourse import mybir

ALU = mybir.AluOpType
ACT = mybir.ActivationFunctionType
F32 = mybir.dt.float32
F16 = mybir.dt.float16
BF16 = mybir.dt.bfloat16
I32 = mybir.dt.int32
AX_X = mybir.AxisListType.X

P = 128
B, S, D = 32, 256, 128
H, E = 512, 8
HC = H // P
TOK = B * S
NT = TOK // P
GT = 4
GW = GT * P
GB = GW // S
SGT = 16
NSG = NT // SGT
NQ = SGT // GT
PAIRS = E * (E - 1) // 2
STRIDE = TOK + P
ROWS = PAIRS * STRIDE + P
TILES = NT + PAIRS - 1
ROW = D + 4
NOTOK = 1 << 20
BUFS = 4
EPS = 1e-5
NEG = -1e30


def adaln_moe_kernel(nc, x, Wg, bg, Wv, bv, Wd, bd, gate_w, gate_b, w1, b1, w2, b2, c, wmod, out):
    x_t = x.rearrange("b (u p) d -> p (b u) d", p=P)
    out_t = out.rearrange("b (u p) d -> p (b u) d", p=P)
    sorted_rows = nc.dram_tensor("sorted_rows", (ROWS, ROW), F32).ap()
    moe_rows = nc.dram_tensor("moe_rows", (TOK, D), F32).ap()
    mod_rows = nc.dram_tensor("mod_rows", (B, 3 * D), F32).ap()
    moe_t = moe_rows.rearrange("(u p) d -> p u d", p=P)

    with ExitStack() as ctx:
        def sb(name, shape, dt=F32):
            return ctx.enter_context(nc.sbuf_tensor(name, shape, dt))

        def sem(name):
            return ctx.enter_context(nc.semaphore(name))

        bank = [ctx.enter_context(nc.psum_tensor(f"bank{i}", [P, 512], F32)) for i in range(8)]

        xs = sb("xs", [P, NT, D])
        w1hi = sb("w1hi", [P, E * H], F16)
        w1lo = sb("w1lo", [P, E * H], F16)
        w2hi = sb("w2hi", [P, E * H], F16)
        w2lo = sb("w2lo", [P, E * H], F16)
        b1row = sb("b1row", [P, E * H], F16)
        b2row = sb("b2row", [P, E * D], F16)
        ones16 = sb("ones16", [P, P], F16)
        ident = sb("ident", [P, P])
        w1f = sb("w1f", [P, E * H])
        w2f = sb("w2f", [P, E * H])
        bstage = sb("bstage", [1, E * H])
        wraw = sb("wraw", [P, 3, D])
        wT = sb("wT", [P, 3, D])
        bcol = sb("bcol", [P, 3])
        bhalf = sb("bhalf", [P, 2])
        gw = sb("gw", [E, D])
        gwT = sb("gwT", [P, E])
        gbias = sb("gbias", [P, E])
        csb = sb("csb", [B, D])
        ctanh = sb("ctanh", [B, D])
        csilu = sb("csilu", [B, D])
        csT = sb("csT", [P, B])
        wmods = sb("wmods", [P, 6 * D])
        sa = sb("sa", [P, B])
        ca1 = sb("ca1", [P, B])
        gasg = sb("gasg", [P, B])
        gaab = sb("gaab", [P, B])
        gaN = sb("gaN", [P, B])
        gabv = sb("gabv", [P, B])
        modr = sb("modr", [B, 3, D])
        gbsg = sb("gbsg", [B, D])
        gbab = sb("gbab", [B, D])
        eps_col = sb("eps_col", [P, 1])
        st1 = sb("st1", [P, NT, 6])
        std1 = sb("std1", [P, NT])
        rstd1 = sb("rstd1", [P, NT])
        nmr1 = sb("nmr1", [P, NT])
        lnt = sb("lnt", [P, 4, NT])
        xn = sb("xn", [P, GW])
        hT = sb("hT", [P, GW])
        a = sb("a", [P, GW])
        tg = sb("tg", [P, GW])
        vs = sb("vs", [P, GW])
        u = sb("u", [P, GW])
        hs = sb("hs", [P, GW])
        r = sb("r", [P, GW])
        st2 = sb("st2", [P, SGT, 6])
        std2 = sb("std2", [P, SGT])
        rstd2 = sb("rstd2", [P, SGT])
        nmr2 = sb("nmr2", [P, SGT])
        pay = sb("pay", [P, SGT, ROW])
        payi = pay[:, :, :].bitcast(I32)
        mb = [sb(f"mb{q}", [P, GB, 2, D]) for q in range(NQ)]
        h2T = sb("h2T", [P, GW])
        L = sb("L", [P, SGT, E])
        Ex = sb("Ex", [P, SGT, E])
        cand = sb("cand", [P, SGT, E])
        oh1 = sb("oh1", [P, SGT, E])
        D2 = sb("D2", [P, SGT, E])
        desc = sb("desc", [P, E])
        small = {n: sb("r_" + n, [P, SGT]) for n in
                 ("m1", "m2", "c1", "c2", "s", "p1", "em2", "p2", "cmax", "cmin", "ehi", "elo", "tri",
                  "pair", "isl", "ish", "t1", "t2", "t3", "t4", "pos")}
        pair_iota = sb("pair_iota", [P, PAIRS])
        OH = sb("OH", [P, SGT, PAIRS], BF16)
        prod = sb("prod", [P, SGT, PAIRS])
        upper = sb("upper", [P, P], BF16)
        ones_bf = sb("ones_bf", [P, P], BF16)
        seen = sb("seen", [P, PAIRS], BF16)
        seen_add = sb("seen_add", [P, PAIRS])
        idx = sb("idx", [P, SGT], I32)
        tok = sb("tok", [P, NT], I32)
        cnt = sb("cnt", [P, PAIRS])
        cnti = sb("cnti", [P, PAIRS], I32)
        cntt = sb("cntt", [P, PAIRS], I32)
        ntl = sb("ntl", [P, PAIRS])
        tend = sb("tend", [P, PAIRS])
        tstart = sb("tstart", [P, PAIRS])
        onesf = sb("onesf", [P, PAIRS])
        le_end = sb("le_end", [P, PAIRS])
        le_start = sb("le_start", [P, PAIRS])
        inpair = sb("inpair", [P, PAIRS])
        tt = sb("tt", [P, 3, PAIRS])
        elo_of = sb("elo_of", [P, PAIRS])
        ehi_of = sb("ehi_of", [P, PAIRS])
        pidx = sb("pidx", [P, 1])
        negin = sb("negin", [P, 1])
        ngone = sb("ngone", [P, 1])
        base0 = sb("base0", [P, 1])
        tcols = sb("tcols", [P, 4])
        table = sb("table", [4, P], I32)
        padrow = sb("padrow", [1, PAIRS], I32)
        region0 = sb("region0", [P, PAIRS])
        padt = sb("padt", [P, ROW])
        xin = [sb(f"xin{k}", [P, ROW]) for k in range(BUFS)]
        meta = [sb(f"meta{k}", [P, 4]) for k in range(BUFS)]
        xh = [sb(f"xh{k}", [P, P], F16) for k in range(2)]
        xl = [sb(f"xl{k}", [P, P], F16) for k in range(2)]
        hh = [[sb(f"hh{k}{e}", [P, H], F16) for e in range(2)] for k in range(2)]
        hl = [[sb(f"hl{k}{e}", [P, H], F16) for e in range(2)] for k in range(2)]
        ylo = [sb(f"ylo{k}", [P, D]) for k in range(2)]
        ysb = [sb(f"ysb{k}", [P, D]) for k in range(BUFS)]
        yin = [w1f[:, q * GW:(q + 1) * GW].rearrange("p (t d) -> p t d", t=GT) for q in range(NQ)]
        yout = [w1f[:, (NQ + q) * GW:(NQ + q + 1) * GW].rearrange("p (t d) -> p t d", t=GT) for q in range(NQ)]
        gin = [w2f[:, q * GB * D:(q + 1) * GB * D].rearrange("p (b d) -> p b d", b=GB) for q in range(NQ)]

        consts_in = sem("consts_in")
        x_in = [sem(f"x_in{s}") for s in range(NSG)]
        w1_in, w2_in = sem("w1_in"), sem("w2_in")
        iota_done = sem("iota_done")
        dve_step, act_step, pool_step = sem("dve_step"), sem("act_step"), sem("pool_step")
        setup_pe, setup_dve, setup_act = sem("setup_pe"), sem("setup_dve"), sem("setup_act")
        w_hi, w_lo = sem("w_hi"), sem("w_lo")
        modrow_out = sem("modrow_out")
        v1_ready, std1_ready = sem("v1_ready"), sem("std1_ready")
        xn_ready, xnT_ready, hT_ready, z_ready = sem("xn_ready"), sem("xnT_ready"), sem("hT_ready"), sem("z_ready")
        z_used, gates_ready, r_ready, rT_ready, x1_ready = (sem("z_used"), sem("gates_ready"), sem("r_ready"),
                                                            sem("rT_ready"), sem("x1_ready"))
        v2_ready, std2_ready, xn2_ready, h2_ready = sem("v2_ready"), sem("std2_ready"), sem("xn2_ready"), sem("h2_ready")
        mb_in = [sem(f"mb_in{q}") for q in range(NQ)]
        h2Tp_ready, h2T_ready, lg_ready, L_ready = sem("h2Tp_ready"), sem("h2T_ready"), sem("lg_ready"), sem("L_ready")
        d_ready, e_ready, oh_ready, rank_ready, idx_ready = (sem("d_ready"), sem("e_ready"), sem("oh_ready"),
                                                             sem("rank_ready"), sem("idx_ready"))
        scattered = [sem(f"scattered{q}") for q in range(NQ)]
        cnt_ready, tcols_ready, tcolsT_ready, table_ready = (sem("cnt_ready"), sem("tcols_ready"),
                                                             sem("tcolsT_ready"), sem("table_ready"))
        pad_out = sem("pad_out")
        tile_in = [sem(f"tile_in{k}") for k in range(BUFS)]
        xT_ready, xh_ready, xl_ready = sem("xT_ready"), sem("xh_ready"), sem("xl_ready")
        hps_ready, hh_ready, hl_ready = sem("hps_ready"), sem("hh_ready"), sem("hl_ready")
        yps_ready, ylo_ready, ysb_ready = sem("yps_ready"), sem("ylo_ready"), sem("ysb_ready")
        ysc = [sem(f"ysc{k}") for k in range(BUFS)]
        yin_done = [sem(f"yin_done{q}") for q in range(NQ)]
        ymul_ready, yout_ready = sem("ymul_ready"), sem("yout_ready")
        stored = [sem(f"stored{q}") for q in range(NQ)]

        pool_turn, dve_turn = sem("pool_turn"), sem("dve_turn")

        N_CONST = 11
        SETUP_IOTA = 1
        LOOP_TILES = TILES // BUFS * BUFS
        assert TILES - LOOP_TILES >= 2

        block = ctx.enter_context(nc.Block())

        @block.sync
        def _(sp):
            for dst, src in ((csb[:], c), (wmods[:], wmod), (wraw[:, 0, :], Wg), (wraw[:, 1, :], Wd),
                             (wraw[:, 2, :], Wv), (gw[:], gate_w),
                             (bcol[:, 0:1], bg.rearrange("(p o) -> p o", o=1)),
                             (bcol[:, 1:2], bd.rearrange("(p o) -> p o", o=1)),
                             (bcol[:, 2:3], bv.rearrange("(p o) -> p o", o=1)),
                             (gbias[:], gate_b.partition_broadcast(P)),
                             (bstage[:, :], b1.rearrange("(o e) h -> o (e h)", o=1))):
                sp.dma_start(dst, src).then_inc(consts_in, 16)
            for s in range(NSG):
                sp.dma_start(xs[:, s * SGT:(s + 1) * SGT, :], x_t[:, s * SGT:(s + 1) * SGT, :]).then_inc(x_in[s], 16)
                if s == 1:
                    sp.dma_start(w1f[:, :].rearrange("p (e h) -> p e h", e=E), w1.rearrange("e d h -> d e h")
                                 ).then_inc(w1_in, 16)
            sp.dma_start(w2f[:, :].rearrange("p (e c o) -> p e c o", e=E, c=HC),
                         w2.rearrange("e (c p) o -> p e c o", p=P)).then_inc(w2_in, 16)
            sp.wait_ge(setup_dve, 5)
            sp.dma_start(mod_rows, modr[:, :, :].rearrange("b m d -> b (m d)")).then_inc(modrow_out, 16)
            sp.wait_ge(modrow_out, 16)
            sp.wait_ge(setup_dve, 6)
            sp.dma_start(bstage[:, 0:E * D], b2.rearrange("(o e) d -> o (e d)", o=1)).then_inc(consts_in, 16)
            with sp.Fori(0, NSG) as sg:
                for q in range(NQ):
                    sp.wait_ge(h2_ready, sg * NQ)
                    src = mod_rows[bass.ds(sg * (NQ * GB) + q * GB, GB), 0:2 * D]
                    sp.dma_start(mb[q][:, :, :, :].rearrange("p b m d -> p b (m d)"),
                                 src.partition_broadcast(P)).then_inc(mb_in[q], 16)
            sp.wait_ge(table_ready, 1)
            with sp.Fori(0, PAIRS) as j:
                row = sp.value_load(padrow[0:1, bass.ds(j, 1)], min_val=0, max_val=ROWS - P)
                sp.dma_start(sorted_rows[bass.ds(row, P), :], padt[:, :]).then_inc(pad_out, 16)
            sp.dma_start(sorted_rows[PAIRS * STRIDE:ROWS, :], padt[:, :]).then_inc(pad_out, 16)
            sp.wait_ge(pad_out, 16 * (PAIRS + 1))
            for q in range(NQ):
                sp.wait_ge(scattered[q], 16 * GT * NSG)

            def load_tile(it, k4):
                k = k4 % BUFS
                row = sp.value_load(table[0:1, bass.ds(it * BUFS + k4, 1)], min_val=0, max_val=ROWS - P)
                sp.dma_start(xin[k][:, :], sorted_rows[bass.ds(row, P), :]).then_inc(tile_in[k], 16)

            for i in range(BUFS):
                load_tile(0, i)
            with sp.Fori(0, LOOP_TILES // BUFS - 1) as it:
                for k in range(BUFS):
                    sp.wait_ge(xl_ready, it * (2 * BUFS) + 2 * k + 2)
                    load_tile(it, k + BUFS)
            for i in range(LOOP_TILES, TILES):
                sp.wait_ge(xl_ready, 2 * (i - BUFS) + 2)
                load_tile(0, i)
            for k in range(BUFS):
                sp.wait_ge(ysc[k], 16 * len(range(k, TILES, BUFS)))
            with sp.Fori(0, NSG) as sg:
                for q in range(NQ):
                    g = sg * NQ + q
                    sp.wait_ge(yout_ready, sg * NQ)
                    sp.dma_start(yin[q][:, :, :], moe_t[:, bass.ds(sg * SGT + q * GT, GT), :]).then_inc(yin_done[q], 16)
                    sp.dma_start(gin[q][:, :, :],
                                 mod_rows[bass.ds(sg * (NQ * GB) + q * GB, GB), 2 * D:3 * D].partition_broadcast(P)
                                 ).then_inc(yin_done[q], 16)

        @block.gpsimd
        def _(pool):
            done = 0

            def mark(ins):
                nonlocal done
                done += 1
                ins.then_inc(pool_step, 1)

            def join():
                pool.wait_ge(pool_step, done)

            for t in (ones16, ones_bf, onesf, upper):
                mark(pool.memset(t[:, :], 1.0))
            for t in (ident, b1row, b2row, seen, padt):
                mark(pool.memset(t[:, :], 0.0))
            mark(pool.memset(eps_col[:, :], EPS))
            mark(pool.memset(pay[:, :, D:ROW], 0.0))
            mark(pool.iota(tok[:, :], pattern=[[P, NT]], base=0, channel_multiplier=1))
            mark(pool.iota(cntt[:, :], pattern=[[1, PAIRS]], base=0, channel_multiplier=0))
            mark(pool.iota(cnti[:, 0:1], pattern=[[0, 1]], base=0, channel_multiplier=1))
            mark(pool.iota(cnti[:, E:2 * E], pattern=[[-1, E]], base=E, channel_multiplier=0))
            join()
            mark(pool.memset(padt[:, D + 2:D + 3].bitcast(I32), NOTOK))
            mark(pool.affine_select(out=ident[:, :], in_=ident[:, :], compare_op=ALU.not_equal, fill=1.0, base=0,
                                    pattern=[[-1, P]], channel_multiplier=1))
            mark(pool.affine_select(out=upper[:, :], in_=upper[:, :], compare_op=ALU.is_gt, fill=0.0, base=0,
                                    pattern=[[1, P]], channel_multiplier=-1))
            mark(pool.tensor_copy(pair_iota[:, :], cntt[:, :]))
            mark(pool.tensor_copy(pidx[:, :], cnti[:, 0:1]))
            mark(pool.tensor_copy(desc[:, :], cnti[:, E:2 * E]))
            join()
            mark(pool.tensor_scalar(region0[:, :], pair_iota[:, :], float(STRIDE), None, ALU.mult))
            for hi in range(1, E):
                first = hi * (hi - 1) // 2
                mark(pool.memset(ehi_of[:, first:first + hi], float(hi)))
                mark(pool.tensor_scalar(elo_of[:, first:first + hi], pair_iota[:, first:first + hi], float(first),
                                        None, ALU.subtract))
            join()
            pool.memset(cnti[:, 0:1], 0).then_inc(iota_done, 1)
            for n, (f, hi, lo) in enumerate(((w1f, w1hi, w1lo), (w2f, w2hi, w2lo))):
                pool.wait_ge(w_hi, n + 1)
                pool.tensor_tensor(lo[:, :], f[:, :], hi[:, :], ALU.subtract).then_inc(w_lo, 1)

            with pool.Fori(0, NSG) as sg:
                for q in range(NQ):
                    pv = pay[:, q * GT:(q + 1) * GT, 0:D].rearrange("p (b t) d -> p b t d", b=GB)
                    pool.wait_ge(xn2_ready, sg * NQ + q + 1)
                    pool.wait_ge(mb_in[q], sg * 16 + 16)
                    pool.sem_inc(pool_turn, 1)

                    def row(m):
                        return mb[q][:, :, m, :].unsqueeze(2).to_broadcast([P, GB, GT // GB, D])
                    pool.tensor_tensor(pv, pv, row(1), ALU.mult).then_inc(pool_step, 1)
                    pool.wait_ge(pool_step, sg * NQ + q + 1 + done)
                    pool.sem_inc(pool_turn, 1)
                    pool.tensor_tensor(pv, pv, row(0), ALU.add).then_inc(h2_ready, 1)
                pool.wait_ge(idx_ready, sg + 1)
                pool.sem_inc(pool_turn, 1)
                for j in range(SGT):
                    pool.indirect_dma_start(sorted_rows, bass.IndirectOffsetOnAxis(idx[:, j:j + 1], 0),
                                            pay[:, j, :], None).then_inc(scattered[j // GT], 16)

            def scatter_tile(it, k4):
                k = k4 % BUFS
                pool.wait_ge(ysb_ready, it * BUFS + k4 + 1)
                pool.sem_inc(pool_turn, 1)
                pool.indirect_dma_start(moe_rows, bass.IndirectOffsetOnAxis(meta[k][:, 2:3].bitcast(I32), 0),
                                        ysb[k][:, :], None, bounds_check=TOK - 1, oob_is_err=False
                                        ).then_inc(ysc[k], 16)

            with pool.Fori(0, LOOP_TILES // BUFS) as it:
                for k in range(BUFS):
                    scatter_tile(it, k)
            for i in range(LOOP_TILES, TILES):
                scatter_tile(0, i)
            with pool.Fori(0, NSG) as sg:
                for q in range(NQ):
                    pool.wait_ge(yin_done[q], sg * 32 + 32)
                    pool.sem_inc(pool_turn, 1)
                    yv = yin[q][:, :, :].rearrange("p (b t) d -> p b t d", b=GB)
                    pool.tensor_tensor(yv, yv, gin[q][:, :, :].unsqueeze(2).to_broadcast([P, GB, GT // GB, D]),
                                       ALU.mult).then_inc(ymul_ready, 1)

        @block.scalar
        def _(act):
            act.wait_ge(consts_in, 16 * N_CONST)
            act.activation(ctanh[:, :], csb[:, :], ACT.Tanh, scale=0.5).then_inc(setup_act, 1)
            act.wait_ge(v1_ready, 1)
            act.wait_ge(iota_done, 1)
            act.activation(std1[:, :], lnt[:, 3, :], ACT.Sqrt, bias=eps_col[:, 0:1], scale=1.0 / D
                           ).then_inc(std1_ready, 1)
            for n, (arrived, f, hi) in enumerate(((w1_in, w1f, w1hi), (w2_in, w2f, w2hi))):
                act.wait_ge(arrived, 16)
                act.activation(hi[:, :], f[:, :], ACT.Copy).then_inc(w_hi, 1)
            act.wait_ge(setup_dve, 5)

            with act.Fori(0, NSG) as sg:
                for q in range(NQ):
                    g = sg * NQ + q
                    act.wait_ge(xnT_ready, g + 1)
                    act.wait_ge(z_ready, g)
                    for b in range(GB):
                        bb = g * GB + b
                        ins = act.activation(hT[:, b * S:(b + 1) * S], bank[0][:, b * S:(b + 1) * S], ACT.Identity,
                                             bias=sa[:, bass.ds(bb, 1)], scale=ca1[:, bass.ds(bb, 1)])
                    ins.then_inc(hT_ready, 1)
                    act.wait_ge(z_ready, g + 1)
                    act.wait_ge(r_ready, g)
                    act.activation(a[:, :], bank[2][:, :], ACT.Tanh, bias=bhalf[:, 1:2], scale=0.5
                                   ).then_inc(act_step, 1)
                    for b in range(GB):
                        bb = g * GB + b
                        act.activation(vs[:, b * S:(b + 1) * S], bank[3][:, b * S:(b + 1) * S], ACT.Identity,
                                       bias=gabv[:, bass.ds(bb, 1)], scale=gaN[:, bass.ds(bb, 1)])
                    act.activation(tg[:, :], bank[1][:, :], ACT.Tanh, bias=bhalf[:, 0:1], scale=0.5
                                   ).then_inc(z_used, 1)
                    act.wait_ge(act_step, g + 1)
                    act.activation(a[:, :], a[:, :], ACT.Copy, bias=0.5, scale=0.5).then_inc(gates_ready, 1)
                act.wait_ge(v2_ready, sg + 1)
                act.activation(std2[:, :], lnt[:, 3, 0:SGT], ACT.Sqrt, bias=eps_col[:, 0:1], scale=1.0 / D
                               ).then_inc(std2_ready, 1)
                for q in range(NQ):
                    g = sg * NQ + q
                    act.wait_ge(h2Tp_ready, g + 1)
                    act.wait_ge(lg_ready, g)
                    act.activation(h2T[:, :], bank[5][:, :], ACT.Copy).then_inc(h2T_ready, 1)
                act.wait_ge(d_ready, sg + 1)
                act.activation(Ex[:, :, :], L[:, :, :], ACT.Exp)
                act.activation(small["em2"][:, :], small["m2"][:, :], ACT.Exp).then_inc(e_ready, 1)

            def x_high(it, n):
                i = it * BUFS + n
                act.wait_ge(xT_ready, i + 1)
                if not (isinstance(it, int) and i < 2):
                    act.wait_ge(hps_ready, it * (2 * BUFS) + (2 * n - 2))
                act.activation(xh[n % 2][:, :], bank[4 + n % 2][:, 0:P], ACT.Copy).then_inc(xh_ready, 1)

            def h_high(it, n):
                i = it * BUFS + n
                for e in range(2):
                    act.wait_ge(hps_ready, i * 2 + e + 1)
                    if not (isinstance(it, int) and i < 2):
                        act.wait_ge(yps_ready, it * BUFS + (n - 1))
                    act.activation(hh[n % 2][e][:, :], bank[2 * (n % 2) + e][:, :], ACT.Relu).then_inc(hh_ready, 1)

            def y_low(it, n):
                i = it * BUFS + n
                act.wait_ge(yps_ready, i + 1)
                if not (isinstance(it, int) and i < 2):
                    act.wait_ge(ysb_ready, it * BUFS + (n - 1))
                act.activation(ylo[n % 2][:, :], bank[6 + n % 2][:, 0:D], ACT.Copy,
                               scale=meta[n % BUFS][:, 0:1]).then_inc(ylo_ready, 1)

            x_high(0, 0)
            x_high(0, 1)
            h_high(0, 0)
            x_high(0, 2)
            h_high(0, 1)
            y_low(0, 0)
            with act.Fori(0, LOOP_TILES // BUFS) as it:
                for k in range(2, BUFS + 2):
                    x_high(it, k + 1)
                    h_high(it, k)
                    y_low(it, k - 1)
            for i in range(LOOP_TILES + 2, TILES):
                if i + 1 < TILES:
                    x_high(0, i + 1)
                h_high(0, i)
                y_low(0, i - 1)
            y_low(0, TILES - 1)
            with act.Fori(0, NSG) as sg:
                for q in range(NQ):
                    act.wait_ge(yout_ready, sg * NQ + q + 1)
                    act.dma_start(out_t[:, bass.ds(sg * SGT + q * GT, GT), :], yout[q][:, :, :]).then_inc(stored[q], 16)
            for q in range(NQ):
                act.wait_ge(stored[q], 16 * NSG)

        @block.vector
        def _(dve):
            base, steps = 0, 0

            def mark(ins):
                nonlocal steps
                ins.then_inc(dve_step, 1)
                steps += 1

            def join():
                dve.wait_ge(dve_step, base + steps)

            def step(ins):
                mark(ins)
                join()

            def signed_clamp(dst, sg_t, ab_t, src):
                step(dve.tensor_copy(dst, src))
                mark(dve.tensor_scalar(sg_t, dst, 0.0, 2.0, ALU.is_ge, ALU.mult))
                step(dve.tensor_scalar(ab_t, dst, -1.0, 0.25, ALU.mult, ALU.max))
                step(dve.tensor_tensor(ab_t, ab_t, dst, ALU.max))
                return dve.scalar_tensor_tensor(out=dst, in0=sg_t, scalar=1.0, in1=ab_t, op0=ALU.subtract, op1=ALU.mult)

            def variances(st, n):
                m0, M0, m1, M1 = (st[:, 0:n, i] for i in (1, 2, 4, 5))
                mark(dve.tensor_tensor(lnt[:, 0, 0:n], m0, m1, ALU.add))
                mark(dve.tensor_tensor(lnt[:, 1, 0:n], m0, m1, ALU.subtract))
                step(dve.tensor_tensor(lnt[:, 2, 0:n], M0, M1, ALU.add))
                step(dve.tensor_tensor(lnt[:, 1, 0:n], lnt[:, 1, 0:n], lnt[:, 1, 0:n], ALU.mult))
                return dve.scalar_tensor_tensor(out=lnt[:, 3, 0:n], in0=lnt[:, 1, 0:n], scalar=D / 4.0,
                                                in1=lnt[:, 2, 0:n], op0=ALU.mult, op1=ALU.add)

            def scales(std, rstd, nmr, n):
                step(dve.reciprocal(rstd[:, 0:n], std[:, 0:n]))
                step(dve.scalar_tensor_tensor(out=nmr[:, 0:n], in0=lnt[:, 0, 0:n], scalar=-0.5, in1=rstd[:, 0:n],
                                              op0=ALU.mult, op1=ALU.mult))

            dve.wait_ge(consts_in, 16 * N_CONST)
            dve.wait_ge(iota_done, 1)
            mark(dve.tensor_scalar(bhalf[:, :], bcol[:, 0:2], 0.5, None, ALU.mult))
            dve.wait_ge(setup_act, 1)
            step(dve.scalar_tensor_tensor(out=csilu[:, :], in0=ctanh[:, :], scalar=1.0, in1=csb[:, :],
                                          op0=ALU.add, op1=ALU.mult))
            dve.tensor_scalar(csilu[:, :], csilu[:, :], 0.5, None, ALU.mult).then_inc(setup_dve, 1)
            dve.wait_ge(setup_pe, 1)
            dve.tensor_copy(csT[:, :], bank[0][:, 0:B]).then_inc(setup_dve, 1)
            dve.wait_ge(setup_pe, 2)
            dve.tensor_copy(wT[:, :, :], bank[1][:, 0:3 * D].rearrange("p (m d) -> p m d", m=3))
            dve.tensor_copy(gwT[:, :], bank[2][:, 0:E]).then_inc(setup_dve, 1)
            dve.wait_ge(setup_pe, 3)
            mark(dve.tensor_copy(sa[:, :], bank[3][:, 0:B]))
            mark(dve.tensor_scalar(ca1[:, :], bank[3][:, B:2 * B], 1.0, None, ALU.add))
            step(signed_clamp(gaN[:, :], gasg[:, :], gaab[:, :], bank[3][:, 2 * B:3 * B]))
            step(dve.tensor_scalar(gaN[:, :], gaN[:, :], -0.5, None, ALU.mult))
            dve.tensor_scalar(gabv[:, :], gaN[:, :], bcol[:, 2:3], None, ALU.mult).then_inc(setup_dve, 1)
            dve.tensor_copy(modr[:, 0, :], bank[4][0:B, 0:D])
            dve.tensor_scalar(modr[:, 1, :], bank[4][0:B, D:2 * D], 1.0, None, ALU.add)
            signed_clamp(modr[:, 2, :], gbsg[:, :], gbab[:, :], bank[4][0:B, 2 * D:3 * D]).then_inc(setup_dve, 1)
            step(dve.tensor_copy(b1row[0:1, :], bstage[:, :]))
            dve.tensor_tensor(b1row[32:33, :], bstage[:, :], b1row[0:1, :], ALU.subtract).then_inc(setup_dve, 1)
            for s in range(NSG):
                dve.wait_ge(x_in[s], 16)
                with dve.Fori(0, SGT // GT) as t4:
                    for k in range(GT):
                        t = t4 * GT + (s * SGT + k)
                        dve.bn_stats(st1[:, bass.ds(t, 1), :].rearrange("p o s -> p (o s)"),
                                     xs[:, bass.ds(t, 1), :].rearrange("p o d -> p (o d)")).then_inc(dve_step, 1)
                steps += SGT
            join()
            variances(st1, NT).then_inc(v1_ready, 1)
            dve.wait_ge(std1_ready, 1)
            scales(std1, rstd1, nmr1, NT)
            dve.wait_ge(consts_in, 16 * (N_CONST + 1))
            step(dve.tensor_copy(b2row[0:1, :], bstage[:, 0:E * D]))
            step(dve.tensor_tensor(b2row[32:33, :], bstage[:, 0:E * D], b2row[0:1, :], ALU.subtract))

            start, steps = steps, 0
            steps_per_sg = 50
            m = {n: t[:, :] for n, t in small.items()}

            def wide(t2, n):
                return t2.unsqueeze(2).to_broadcast([P, SGT, n])

            def over_tiles(t2, n):
                return t2.unsqueeze(1).to_broadcast([P, SGT, n])

            with dve.Fori(0, NSG) as sg:
                base = sg * steps_per_sg + start

                def normalize(q):
                    dve.wait_ge(xnT_ready, sg * NQ + q)
                    for j in range(GT):
                        t = sg * SGT + (q * GT + j)
                        ins = dve.tensor_scalar(xn[:, j * P:(j + 1) * P],
                                                xs[:, bass.ds(t, 1), :].rearrange("p o d -> p (o d)"),
                                                rstd1[:, bass.ds(t, 1)], nmr1[:, bass.ds(t, 1)], ALU.mult, ALU.add)
                    ins.then_inc(xn_ready, 1)

                normalize(0)
                for q in range(NQ):
                    g = sg * NQ + q
                    if q + 1 < NQ:
                        normalize(q + 1)
                    dve.wait_ge(gates_ready, g + 1)
                    step(dve.scalar_tensor_tensor(out=u[:, :], in0=a[:, :], scalar=1.0, in1=vs[:, :],
                                                  op0=ALU.subtract, op1=ALU.mult))
                    for b in range(GB):
                        half = slice(b * S, (b + 1) * S)
                        mark(dve.tensor_tensor_scan(hs[:, half], a[:, half], u[:, half], 0.0, ALU.mult, ALU.add))
                    join()
                    dve.wait_ge(rT_ready, g)
                    dve.scalar_tensor_tensor(out=r[:, :], in0=tg[:, :], scalar=1.0, in1=hs[:, :],
                                             op0=ALU.add, op1=ALU.mult).then_inc(r_ready, 1)
                    dve.wait_ge(rT_ready, g + 1)
                    xg = xs[:, bass.ds(sg * SGT + q * GT, GT), :]
                    dve.tensor_tensor(xg, bank[4][:, :].rearrange("p (t d) -> p t d", t=GT), xg,
                                      ALU.add).then_inc(x1_ready, 1)
                    dve.wait_ge(x1_ready, g + 1)
                    dve.sem_inc(dve_turn, 1)
                    for j in range(GT):
                        t = sg * SGT + (q * GT + j)
                        ins = dve.bn_stats(st2[:, q * GT + j, :], xs[:, bass.ds(t, 1), :].rearrange("p o d -> p (o d)"))
                step(ins)
                variances(st2, SGT).then_inc(v2_ready, 1)
                dve.wait_ge(std2_ready, sg + 1)
                scales(std2, rstd2, nmr2, SGT)
                for q in range(NQ):
                    dve.wait_ge(scattered[q], sg * (16 * GT))
                    for j in range(q * GT, (q + 1) * GT):
                        ins = dve.tensor_scalar(pay[:, j, 0:D],
                                                xs[:, bass.ds(sg * SGT + j, 1), :].rearrange("p o d -> p (o d)"),
                                                rstd2[:, j:j + 1], nmr2[:, j:j + 1], ALU.mult, ALU.add)
                    ins.then_inc(xn2_ready, 1)
                dve.wait_ge(lg_ready, sg * NQ + NQ)
                dve.tensor_tensor(L[:, :, :], bank[6][:, 0:SGT * E].rearrange("p (t e) -> p t e", e=E),
                                  over_tiles(gbias[:, :], E), ALU.add).then_inc(L_ready, 1)
                dve.wait_ge(L_ready, sg + 1)
                step(dve.tensor_reduce(m["m1"], L[:, :, :], AX_X, ALU.max))
                step(dve.tensor_tensor(L[:, :, :], L[:, :, :], wide(m["m1"], E), ALU.subtract))
                step(dve.scalar_tensor_tensor(out=cand[:, :, :], in0=L[:, :, :], scalar=0.0,
                                              in1=over_tiles(desc[:, :], E), op0=ALU.is_equal, op1=ALU.mult))
                step(dve.tensor_reduce(m["c1"], cand[:, :, :], AX_X, ALU.max))
                step(dve.tensor_tensor(oh1[:, :, :], over_tiles(desc[:, :], E), wide(m["c1"], E), ALU.is_equal))
                step(dve.scalar_tensor_tensor(out=D2[:, :, :], in0=oh1[:, :, :], scalar=NEG, in1=L[:, :, :],
                                              op0=ALU.mult, op1=ALU.add))
                dve.tensor_reduce(m["m2"], D2[:, :, :], AX_X, ALU.max).then_inc(d_ready, 1)
                dve.wait_ge(d_ready, sg + 1)
                step(dve.tensor_tensor(cand[:, :, :], D2[:, :, :], wide(m["m2"], E), ALU.is_equal))
                step(dve.tensor_tensor(cand[:, :, :], cand[:, :, :], over_tiles(desc[:, :], E), ALU.mult))
                step(dve.tensor_reduce(m["c2"], cand[:, :, :], AX_X, ALU.max))
                mark(dve.tensor_tensor(m["cmax"], m["c1"], m["c2"], ALU.max))
                mark(dve.tensor_tensor(m["cmin"], m["c1"], m["c2"], ALU.min))
                mark(dve.tensor_tensor(m["isl"], m["c1"], m["c2"], ALU.is_gt))
                step(dve.tensor_tensor(m["ish"], m["c1"], m["c2"], ALU.is_lt))
                mark(dve.tensor_scalar(m["elo"], m["cmax"], -1.0, float(E), ALU.mult, ALU.add))
                step(dve.tensor_scalar(m["ehi"], m["cmin"], -1.0, float(E), ALU.mult, ALU.add))
                step(dve.scalar_tensor_tensor(out=m["tri"], in0=m["ehi"], scalar=1.0, in1=m["ehi"],
                                              op0=ALU.subtract, op1=ALU.mult))
                step(dve.scalar_tensor_tensor(out=m["pair"], in0=m["tri"], scalar=0.5, in1=m["elo"],
                                              op0=ALU.mult, op1=ALU.add))
                dve.tensor_tensor(OH[:, :, :], over_tiles(pair_iota[:, :], PAIRS), wide(m["pair"], PAIRS),
                                  ALU.is_equal).then_inc(oh_ready, 1)
                dve.wait_ge(e_ready, sg + 1)
                step(dve.tensor_reduce(m["s"], Ex[:, :, :], AX_X, ALU.add))
                step(dve.reciprocal(m["p1"], m["s"]))
                step(dve.tensor_tensor(m["p2"], m["em2"], m["p1"], ALU.mult))
                mark(dve.tensor_tensor(m["t1"], m["isl"], m["p1"], ALU.mult))
                mark(dve.tensor_tensor(m["t2"], m["ish"], m["p2"], ALU.mult))
                mark(dve.tensor_tensor(m["t3"], m["ish"], m["p1"], ALU.mult))
                step(dve.tensor_tensor(m["t4"], m["isl"], m["p2"], ALU.mult))
                mark(dve.tensor_tensor(pay[:, :, D], m["t1"], m["t2"], ALU.add))
                mark(dve.tensor_tensor(pay[:, :, D + 1], m["t3"], m["t4"], ALU.add))
                mark(dve.tensor_copy(payi[:, :, D + 2], tok[:, bass.ds(sg * SGT, SGT)]))
                dve.wait_ge(oh_ready, sg + 1)
                step(dve.tensor_reduce(seen_add[:, :], OH[:, :, :].rearrange("p t j -> p j t"), AX_X, ALU.add))
                dve.wait_ge(rank_ready, sg + 1)
                mark(dve.tensor_tensor(seen[:, :], seen[:, :], seen_add[:, :], ALU.add))
                step(dve.tensor_tensor(prod[:, :, :], bank[7][:, 0:SGT * PAIRS].rearrange("p (t j) -> p t j", j=PAIRS),
                                       OH[:, :, :], ALU.mult))
                step(dve.tensor_reduce(m["pos"], prod[:, :, :], AX_X, ALU.add))
                dve.scalar_tensor_tensor(out=idx[:, :], in0=m["pair"], scalar=float(STRIDE), in1=m["pos"],
                                         op0=ALU.mult, op1=ALU.add).then_inc(idx_ready, 1)
            assert steps == steps_per_sg, steps
            base, steps = start + NSG * steps_per_sg, 0
            dve.wait_ge(cnt_ready, 1)
            step(dve.tensor_copy(cnt[:, :], bank[6][:, 0:PAIRS]))
            mark(dve.tensor_tensor(padrow[:, :], cnt[0:1, :], region0[0:1, :], ALU.add))
            step(dve.tensor_scalar(cnti[:, :], cnt[:, :], float(P - 1), None, ALU.add))
            step(dve.tensor_scalar(cntt[:, :], cnti[:, :], 7, None, ALU.arith_shift_right))
            step(dve.tensor_copy(ntl[:, :], cntt[:, :]))
            step(dve.tensor_tensor_scan(tend[:, :], onesf[:, :], ntl[:, :], 0.0, ALU.mult, ALU.add))
            mark(dve.tensor_scalar(le_end[:, :], tend[:, :], pidx[:, 0:1], None, ALU.is_le))
            step(dve.tensor_tensor(tstart[:, :], tend[:, :], ntl[:, :], ALU.subtract))
            step(dve.tensor_scalar(le_start[:, :], tstart[:, :], pidx[:, 0:1], None, ALU.is_le))
            step(dve.tensor_tensor(inpair[:, :], le_start[:, :], le_end[:, :], ALU.subtract))
            mark(dve.scalar_tensor_tensor(out=tt[:, 0, :], in0=tstart[:, :], scalar=pidx[:, 0:1], in1=inpair[:, :],
                                          op0=ALU.subtract, op1=ALU.mult))
            mark(dve.tensor_tensor(tt[:, 1, :], inpair[:, :], elo_of[:, :], ALU.mult))
            step(dve.tensor_tensor(tt[:, 2, :], inpair[:, :], ehi_of[:, :], ALU.mult))
            mark(dve.tensor_reduce(ngone[:, :], le_end[:, :], AX_X, ALU.add))
            mark(dve.tensor_copy(tcols[:, 3:4], pidx[:, :]))
            step(dve.tensor_reduce(tcols[:, 0:3], tt[:, :, :], AX_X, ALU.add))
            step(dve.tensor_scalar(base0[:, :], ngone[:, :], float(STRIDE), None, ALU.mult))
            dve.scalar_tensor_tensor(out=tcols[:, 0:1], in0=tcols[:, 0:1], scalar=-float(P), in1=base0[:, :],
                                     op0=ALU.mult, op1=ALU.add).then_inc(tcols_ready, 1)
            dve.wait_ge(tcolsT_ready, 1)
            dve.tensor_copy(table[:, :], bank[6][0:4, 0:P]).then_inc(table_ready, 1)

            def x_low(it, n):
                i = it * BUFS + n
                k = n % BUFS
                dve.wait_ge(tile_in[k], (it + n // BUFS) * 16 + 16)
                if not (isinstance(it, int) and i < BUFS):
                    dve.wait_ge(ysc[k], (it + n // BUFS) * 16)
                dve.tensor_copy(meta[k][:, :], xin[k][:, D:ROW]).then_inc(xl_ready, 1)
                dve.wait_ge(xh_ready, i + 1)
                dve.tensor_tensor(xl[n % 2][:, :], bank[4 + n % 2][:, 0:P], xh[n % 2][:, :], ALU.subtract
                                  ).then_inc(xl_ready, 1)

            def h_low(it, n):
                i = it * BUFS + n
                for e in range(2):
                    dve.wait_ge(hh_ready, i * 2 + e + 1)
                    dve.scalar_tensor_tensor(out=hl[n % 2][e][:, :], in0=bank[2 * (n % 2) + e][:, :], scalar=0.0,
                                             in1=hh[n % 2][e][:, :], op0=ALU.max, op1=ALU.subtract
                                             ).then_inc(hl_ready, 1)

            def y_sum(it, n):
                i = it * BUFS + n
                k = n % BUFS
                dve.wait_ge(ylo_ready, i + 1)
                dve.scalar_tensor_tensor(out=ysb[k][:, :], in0=bank[6 + n % 2][:, D:2 * D], scalar=meta[k][:, 1:2],
                                         in1=ylo[n % 2][:, :], op0=ALU.mult, op1=ALU.add).then_inc(ysb_ready, 1)

            x_low(0, 0)
            x_low(0, 1)
            h_low(0, 0)
            x_low(0, 2)
            h_low(0, 1)
            y_sum(0, 0)
            with dve.Fori(0, LOOP_TILES // BUFS) as it:
                for k in range(2, BUFS + 2):
                    x_low(it, k + 1)
                    h_low(it, k)
                    y_sum(it, k - 1)
            for i in range(LOOP_TILES + 2, TILES):
                if i + 1 < TILES:
                    x_low(0, i + 1)
                h_low(0, i)
                y_sum(0, i - 1)
            y_sum(0, TILES - 1)
            with dve.Fori(0, NSG) as sg:
                for q in range(NQ):
                    dve.wait_ge(ymul_ready, sg * NQ + q + 1)
                    dve.wait_ge(stored[q], sg * 16)
                    dve.tensor_tensor(yout[q][:, :, :], yin[q][:, :, :], xs[:, bass.ds(sg * SGT + q * GT, GT), :],
                                      ALU.add).then_inc(yout_ready, 1)

        @block.tensor
        def _(pe):
            pe.wait_ge(consts_in, 16 * N_CONST)
            pe.wait_ge(iota_done, 1)
            pe.wait_ge(setup_dve, 1)
            pe.transpose(bank[0][:, 0:B], csilu[:, :], ident[0:B, 0:B]).then_inc(setup_pe, 1)
            for i in range(3):
                pe.transpose(bank[1][:, i * D:(i + 1) * D], wraw[:, i, :], ident[:, :])
            pe.transpose(bank[2][:, 0:E], gw[:, :], ident[0:E, 0:E]).then_inc(setup_pe, 1)
            pe.wait_ge(setup_dve, 2)
            for i in range(3):
                pe.matmul(bank[3][:, i * B:(i + 1) * B], wmods[:, i * D:(i + 1) * D], csT[:, :], start=True, stop=True)
            pe.matmul(bank[4][0:B, 0:3 * D], csT[:, :], wmods[:, 3 * D:6 * D], start=True, stop=True).then_inc(setup_pe, 1)
            pe.wait_ge(setup_dve, 3)

            with pe.Fori(0, NSG) as sg:
                for q in range(NQ):
                    g = sg * NQ + q
                    pe.wait_ge(xn_ready, g + 1)
                    pe.wait_ge(hT_ready, g)
                    for j in range(GT):
                        ins = pe.transpose(bank[0][:, j * P:(j + 1) * P], xn[:, j * P:(j + 1) * P], ident[:, :])
                    ins.then_inc(xnT_ready, 1)
                    pe.wait_ge(hT_ready, g + 1)
                    pe.wait_ge(z_used, g)
                    for i in (1, 2, 0):
                        ins = pe.matmul(bank[1 + i][:, :], wT[:, i, :], hT[:, :], start=True, stop=True)
                    ins.then_inc(z_ready, 1)
                    pe.wait_ge(r_ready, g + 1)
                    pe.wait_ge(x1_ready, g)
                    for j in range(GT):
                        ins = pe.transpose(bank[4][:, j * P:(j + 1) * P], r[:, j * P:(j + 1) * P], ident[:, :])
                    ins.then_inc(rT_ready, 1)
                pe.wait_ge(L_ready, sg)
                for q in range(NQ):
                    g = sg * NQ + q
                    pe.wait_ge(h2_ready, g + 1)
                    pe.wait_ge(h2T_ready, g)
                    for j in range(GT):
                        ins = pe.transpose(bank[5][:, j * P:(j + 1) * P], pay[:, q * GT + j, 0:D], ident[:, :])
                    ins.then_inc(h2Tp_ready, 1)
                    pe.wait_ge(h2T_ready, g + 1)
                    for j in range(GT):
                        o = (q * GT + j) * E
                        ins = pe.matmul(bank[6][:, o:o + E], h2T[:, j * P:(j + 1) * P], gwT[:, :], start=True, stop=True)
                    ins.then_inc(lg_ready, 1)
                pe.wait_ge(oh_ready, sg + 1)
                pe.wait_ge(idx_ready, sg)
                ohf = OH[:, :, :].rearrange("p t j -> p (t j)")
                rank = bank[7][:, 0:SGT * PAIRS]
                pe.matmul(rank, upper[:, :], ohf, start=True, stop=False)
                for t in range(1, SGT):
                    pe.matmul(rank[:, t * PAIRS:], ones_bf[:, :], ohf[:, 0:(SGT - t) * PAIRS], start=False, stop=False)
                pe.matmul(rank.rearrange("p (t j) -> p t j", j=PAIRS), ones_bf[:, :],
                          seen[:, :].unsqueeze(1).to_broadcast([P, SGT, PAIRS]), start=False, stop=True
                          ).then_inc(rank_ready, 1)
            pe.wait_ge(idx_ready, NSG)
            pe.matmul(bank[6][:, 0:PAIRS], ones_bf[:, :], seen[:, :], start=True, stop=True).then_inc(cnt_ready, 1)
            pe.wait_ge(tcols_ready, 1)
            pe.transpose(bank[6][0:4, 0:P], tcols[:, :], ident[:, :]).then_inc(tcolsT_ready, 1)
            pe.wait_ge(table_ready, 1)
            pe.wait_ge(w_lo, 2)

            def turn(it, n):
                i = it * BUFS + n
                k = n % BUFS
                pe.wait_ge(tile_in[k], (it + n // BUFS) * 16 + 16)
                if not (isinstance(it, int) and i < 2):
                    pe.wait_ge(xl_ready, it * (2 * BUFS) + (2 * n - 2))
                pe.transpose(bank[4 + n % 2][:, 0:P], xin[k][:, 0:D], ident[:, :]).then_inc(xT_ready, 1)

            def layer1(it, n, experts):
                i = it * BUFS + n
                pe.wait_ge(xl_ready, i * 2 + 2)
                for e in range(2):
                    if not (isinstance(it, int) and i < 2):
                        pe.wait_ge(hl_ready, it * (2 * BUFS) + (2 * n - 3 + e))
                    ps = bank[2 * (n % 2) + e]
                    for cc in range(HC):
                        o = ps[:, cc * P:(cc + 1) * P]

                        def w(t):
                            return t[:, bass.ds(experts[e] * H + cc * P, P)]
                        pe.matmul(o, w(b1row), ones16[:, :], start=True, stop=False)
                        pe.matmul(o, w(w1hi), xh[n % 2][:, :], start=False, stop=False)
                        pe.matmul(o, w(w1hi), xl[n % 2][:, :], start=False, stop=False)
                        ins = pe.matmul(o, w(w1lo), xh[n % 2][:, :], start=False, stop=True)
                    ins.then_inc(hps_ready, 1)

            def layer2(it, n, experts):
                i = it * BUFS + n
                if not (isinstance(it, int) and i < 2):
                    pe.wait_ge(ysb_ready, it * BUFS + (n - 1))
                for e in range(2):
                    pe.wait_ge(hl_ready, i * 2 + e + 1)
                    o = bank[6 + n % 2][:, e * D:(e + 1) * D]
                    pe.matmul(o, ones16[:, :], b2row[:, bass.ds(experts[e] * D, D)], start=True, stop=False)
                    for cc in range(HC):
                        def w(t):
                            return t[:, bass.ds(experts[e] * H + cc * D, D)]
                        hhc, hlc = (t[n % 2][e][:, cc * P:(cc + 1) * P] for t in (hh, hl))
                        pe.matmul(o, hhc, w(w2hi), start=False, stop=False)
                        pe.matmul(o, hhc, w(w2lo), start=False, stop=False)
                        ins = pe.matmul(o, hlc, w(w2hi), start=False, stop=(cc == HC - 1))
                ins.then_inc(yps_ready, 1)

            def experts_of(it, n):
                return [pe.value_load(table[1 + e:2 + e, bass.ds(it * BUFS + n, 1)], min_val=0, max_val=E - 1)
                        for e in range(2)]

            turn(0, 0)
            turn(0, 1)
            layer1(0, 0, experts_of(0, 0))
            turn(0, 2)
            layer1(0, 1, experts_of(0, 1))
            layer2(0, 0, experts_of(0, 0))
            with pe.Fori(0, LOOP_TILES // BUFS) as it:
                for k in range(2, BUFS + 2):
                    turn(it, k + 1)
                    layer1(it, k, experts_of(it, k))
                    layer2(it, k - 1, experts_of(it, k - 1))
            for i in range(LOOP_TILES + 2, TILES):
                if i + 1 < TILES:
                    turn(0, i + 1)
                layer1(0, i, experts_of(0, i))
                layer2(0, i - 1, experts_of(0, i - 1))
            layer2(0, TILES - 1, experts_of(0, TILES - 1))


_INS = ["L0_attn_x", "L0_attn_Wg", "L0_attn_bg", "L0_attn_Wv", "L0_attn_bv", "L0_attn_Wd", "L0_attn_bd",
        "L0_ffn_gate_w", "L0_ffn_gate_b", "L0_ffn_w1", "L0_ffn_b1", "L0_ffn_w2", "L0_ffn_b2", "L0_c", "L0_wmod"]
_OUTS = [((B, S, D), "float32")]


def kernel(**inputs):
    import numpy as _np
    import concourse.bacc as _bacc
    from concourse import mybir as _mybir
    from concourse.bass_utils import run_bass_kernel_spmd as _run

    nc = _bacc.Bacc("TRN2", target_bir_lowering=False, num_devices=1)
    arrays, args = {}, []
    for name in _INS:
        arr = _np.ascontiguousarray(inputs[name])
        arrays[f"in_{name}_dram"] = arr
        args.append(nc.dram_tensor(f"in_{name}_dram", arr.shape, _mybir.dt.from_np(arr.dtype),
                                   kind="ExternalInput").ap())
    for i, (shape, dtype) in enumerate(_OUTS):
        dt = _mybir.dt.from_np(_np.dtype(dtype))
        args.append(nc.dram_tensor(f"out_{i}_dram", shape, dt, kind="ExternalOutput").ap())
    adaln_moe_kernel(nc, *args)
    res = _run(nc, [arrays], core_ids=[0])
    got = tuple(res.results[0][f"out_{i}_dram"] for i in range(len(_OUTS)))
    return got[0]
```

```python
from contextlib import ExitStack

import concourse.bass as bass
from concourse import mybir

ALU = mybir.AluOpType
ACT = mybir.ActivationFunctionType
F32 = mybir.dt.float32
F16 = mybir.dt.float16
BF16 = mybir.dt.bfloat16
I32 = mybir.dt.int32
AX_X = mybir.AxisListType.X

P = 128
B, S, D = 32, 256, 128
H, E = 512, 8
HC = H // P
TOK = B * S
NT = TOK // P
GT = 4
GW = GT * P
GB = GW // S
SGT = 16
NSG = NT // SGT
NQ = SGT // GT
PAIRS = E * (E - 1) // 2
TW = 256
HALVES = TW // P
STRIDE = TOK + TW
ROWS = PAIRS * STRIDE + TW
ROW = D + 4
NOTOK = 1 << 20
BUFS = 4
EPS = 1e-5
NEG = -1e30


def adaln_moe_kernel(nc, x, Wg, bg, Wv, bv, Wd, bd, gate_w, gate_b, w1, b1, w2, b2, c, wmod, out):
    x_t = x.rearrange("b (u p) d -> p (b u) d", p=P)
    out_t = out.rearrange("b (u p) d -> p (b u) d", p=P)
    sorted_rows = nc.dram_tensor("sorted_rows", (ROWS, ROW), F32).ap()
    moe_rows = nc.dram_tensor("moe_rows", (TOK, D), F32).ap()
    mod_rows = nc.dram_tensor("mod_rows", (B, 3 * D), F32).ap()
    moe_t = moe_rows.rearrange("(u p) d -> p u d", p=P)

    with ExitStack() as ctx:
        def sb(name, shape, dt=F32):
            return ctx.enter_context(nc.sbuf_tensor(name, shape, dt))

        def sem(name):
            return ctx.enter_context(nc.semaphore(name))

        bank = [ctx.enter_context(nc.psum_tensor(f"bank{i}", [P, 512], F32)) for i in range(8)]

        xs = sb("xs", [P, NT, D])
        w1hi = sb("w1hi", [P, E * H], F16)
        w1lo = sb("w1lo", [P, E * H], F16)
        w2hi = sb("w2hi", [P, E * H], F16)
        w2lo = sb("w2lo", [P, E * H], F16)
        b2row = sb("b2row", [P, E * H], F16)
        ones16 = sb("ones16", [P, P], F16)
        ident = sb("ident", [P, P])
        w1f = sb("w1f", [P, E * H])
        w2f = sb("w2f", [P, E * H])
        bstage = sb("bstage", [1, E * D])
        wraw = sb("wraw", [P, 3, D])
        wT = sb("wT", [P, 3, D])
        bcol = sb("bcol", [P, 3])
        bhalf = sb("bhalf", [P, 2])
        gw = sb("gw", [E, D])
        gwT = sb("gwT", [P, E])
        gbias = sb("gbias", [P, E])
        csb = sb("csb", [B, D])
        ctanh = sb("ctanh", [B, D])
        csilu = sb("csilu", [B, D])
        csT = sb("csT", [P, B])
        wmods = sb("wmods", [P, 6 * D])
        sa = sb("sa", [P, B])
        ca1 = sb("ca1", [P, B])
        gasg = sb("gasg", [P, B])
        gaab = sb("gaab", [P, B])
        gaN = sb("gaN", [P, B])
        gabv = sb("gabv", [P, B])
        modr = sb("modr", [B, 3, D])
        gbsg = sb("gbsg", [B, D])
        gbab = sb("gbab", [B, D])
        eps_col = sb("eps_col", [P, 1])
        st1 = sb("st1", [P, NT, 6])
        std1 = sb("std1", [P, NT])
        rstd1 = sb("rstd1", [P, NT])
        nmr1 = sb("nmr1", [P, NT])
        lnt = sb("lnt", [P, 4, NT])
        xn = sb("xn", [P, GW])
        hT = sb("hT", [P, GW])
        a = sb("a", [P, GW])
        tg = sb("tg", [P, GW])
        vs = sb("vs", [P, GW])
        u = sb("u", [P, GW])
        hs = sb("hs", [P, GW])
        r = sb("r", [P, GW])
        st2 = sb("st2", [P, SGT, 6])
        std2 = sb("std2", [P, SGT])
        rstd2 = sb("rstd2", [P, SGT])
        nmr2 = sb("nmr2", [P, SGT])
        pay = sb("pay", [P, SGT, ROW])
        payi = pay[:, :, :].bitcast(I32)
        mb = [sb(f"mb{q}", [P, GB, 2, D]) for q in range(NQ)]
        h2T = sb("h2T", [P, GW])
        L = sb("L", [P, SGT, E])
        Ex = sb("Ex", [P, SGT, E])
        cand = sb("cand", [P, SGT, E])
        oh1 = sb("oh1", [P, SGT, E])
        D2 = sb("D2", [P, SGT, E])
        desc = sb("desc", [P, E])
        small = {n: sb("r_" + n, [P, SGT]) for n in
                 ("m1", "m2", "c1", "c2", "s", "p1", "em2", "p2", "cmax", "cmin", "ehi", "elo", "tri",
                  "pair", "isl", "ish", "t1", "t2", "t3", "t4", "pos")}
        pair_iota = sb("pair_iota", [P, PAIRS])
        OH = sb("OH", [P, SGT, PAIRS], BF16)
        prod = sb("prod", [P, SGT, PAIRS])
        upper = sb("upper", [P, P], BF16)
        ones_bf = sb("ones_bf", [P, P], BF16)
        seen = sb("seen", [P, PAIRS], BF16)
        seen_add = sb("seen_add", [P, PAIRS])
        idx = sb("idx", [P, SGT], I32)
        tok = sb("tok", [P, NT], I32)
        cnt = sb("cnt", [P, PAIRS])
        cnti = sb("cnti", [P, PAIRS], I32)
        cntt = sb("cntt", [P, PAIRS], I32)
        ntl = sb("ntl", [P, PAIRS])
        tend = sb("tend", [P, PAIRS])
        tstart = sb("tstart", [P, PAIRS])
        onesf = sb("onesf", [P, PAIRS])
        le_end = sb("le_end", [P, PAIRS])
        le_start = sb("le_start", [P, PAIRS])
        inpair = sb("inpair", [P, PAIRS])
        tt = sb("tt", [P, 3, PAIRS])
        elo_of = sb("elo_of", [P, PAIRS])
        ehi_of = sb("ehi_of", [P, PAIRS])
        pidx = sb("pidx", [P, 1])
        negin = sb("negin", [P, 1])
        ngone = sb("ngone", [P, 1])
        base0 = sb("base0", [P, 1])
        tcols = sb("tcols", [P, 4])
        table = sb("table", [4, P], I32)
        padrow = sb("padrow", [1, PAIRS], I32)
        region0 = sb("region0", [P, PAIRS])
        padt = sb("padt", [P, HALVES, ROW])
        xin = [sb(f"xin{k}", [P, HALVES, ROW]) for k in range(BUFS)]
        meta = [sb(f"meta{k}", [P, HALVES, 4]) for k in range(BUFS)]
        xh = [sb(f"xh{k}", [P, TW], F16) for k in range(2)]
        xl = [sb(f"xl{k}", [P, TW], F16) for k in range(2)]
        hh = [[sb(f"hh{k}{e}", [P, HC, TW], F16) for e in range(2)] for k in range(2)]
        hl = [[sb(f"hl{k}{e}", [P, HC, TW], F16) for e in range(2)] for k in range(2)]
        hf = [sb(f"hf{e}", [P, HC, TW]) for e in range(2)]
        ylo = sb("ylo", [P, HALVES, D])
        ysb = [sb(f"ysb{k}", [P, HALVES, D]) for k in range(BUFS)]
        b1c = sb("b1c", [E * HC, P])
        b1col = sb("b1col", [P, E * HC])
        bcols = [sb(f"bcols{k}", [P, 2 * HC]) for k in range(2)]
        yin = [w1f[:, q * GW:(q + 1) * GW].rearrange("p (t d) -> p t d", t=GT) for q in range(NQ)]
        yout = [w1f[:, (NQ + q) * GW:(NQ + q + 1) * GW].rearrange("p (t d) -> p t d", t=GT) for q in range(NQ)]
        gin = [w2f[:, q * GB * D:(q + 1) * GB * D].rearrange("p (b d) -> p b d", b=GB) for q in range(NQ)]

        consts_in = sem("consts_in")
        x_in = [sem(f"x_in{s}") for s in range(NSG)]
        w1_in, w2_in = sem("w1_in"), sem("w2_in")
        iota_done = sem("iota_done")
        dve_step, act_step, pool_step = sem("dve_step"), sem("act_step"), sem("pool_step")
        setup_pe, setup_dve, setup_act = sem("setup_pe"), sem("setup_dve"), sem("setup_act")
        w_hi, w_lo = sem("w_hi"), sem("w_lo")
        modrow_out = sem("modrow_out")
        v1_ready, std1_ready = sem("v1_ready"), sem("std1_ready")
        xn_ready, xnT_ready, hT_ready, z_ready = sem("xn_ready"), sem("xnT_ready"), sem("hT_ready"), sem("z_ready")
        z_used, gates_ready, r_ready, rT_ready, x1_ready = (sem("z_used"), sem("gates_ready"), sem("r_ready"),
                                                            sem("rT_ready"), sem("x1_ready"))
        v2_ready, std2_ready, xn2_ready, h2_ready = sem("v2_ready"), sem("std2_ready"), sem("xn2_ready"), sem("h2_ready")
        mb_in = [sem(f"mb_in{q}") for q in range(NQ)]
        h2Tp_ready, h2T_ready, lg_ready, L_ready = sem("h2Tp_ready"), sem("h2T_ready"), sem("lg_ready"), sem("L_ready")
        d_ready, e_ready, oh_ready, rank_ready, idx_ready = (sem("d_ready"), sem("e_ready"), sem("oh_ready"),
                                                             sem("rank_ready"), sem("idx_ready"))
        scattered = [sem(f"scattered{q}") for q in range(NQ)]
        cnt_ready, tcols_ready, tcolsT_ready, table_ready = (sem("cnt_ready"), sem("tcols_ready"),
                                                             sem("tcolsT_ready"), sem("table_ready"))
        pad_out = sem("pad_out")
        tile_in = [sem(f"tile_in{k}") for k in range(BUFS)]
        xT_ready, xh_ready, xl_ready = sem("xT_ready"), sem("xh_ready"), sem("xl_ready")
        hps_ready, hh_ready, hl_ready = sem("hps_ready"), sem("hh_ready"), sem("hl_ready")
        hf_ready, bcols_ready = sem("hf_ready"), sem("bcols_ready")
        yps_ready, ylo_ready, ysb_ready = sem("yps_ready"), sem("ylo_ready"), sem("ysb_ready")
        ysc = [sem(f"ysc{k}") for k in range(BUFS)]
        yin_done = [sem(f"yin_done{q}") for q in range(NQ)]
        ymul_ready, yout_ready = sem("ymul_ready"), sem("yout_ready")
        stored = [sem(f"stored{q}") for q in range(NQ)]

        pool_turn, dve_turn, sp_turn = sem("pool_turn"), sem("dve_turn"), sem("sp_turn")

        N_CONST = 12
        SETUP_IOTA = 1

        def loop_turns(eng):
            return eng.value_load(table[3:4, 0:1], min_val=TOK // TW // BUFS, max_val=(TOK // TW + PAIRS) // BUFS)

        def last_turn(eng):
            return eng.value_load(table[3:4, 1:2], min_val=TOK // TW // BUFS - 1,
                                  max_val=(TOK // TW + PAIRS) // BUFS - 1)

        block = ctx.enter_context(nc.Block())

        @block.sync
        def _(sp):
            for dst, src in ((csb[:], c), (wmods[:], wmod), (wraw[:, 0, :], Wg), (wraw[:, 1, :], Wd),
                             (wraw[:, 2, :], Wv), (gw[:], gate_w),
                             (bcol[:, 0:1], bg.rearrange("(p o) -> p o", o=1)),
                             (bcol[:, 1:2], bd.rearrange("(p o) -> p o", o=1)),
                             (bcol[:, 2:3], bv.rearrange("(p o) -> p o", o=1)),
                             (gbias[:], gate_b.partition_broadcast(P)),
                             (b1c[:, :], b1.rearrange("e (c p) -> (e c) p", p=P)),
                             (bstage[:, :], b2.rearrange("(o e) d -> o (e d)", o=1))):
                sp.dma_start(dst, src).then_inc(consts_in, 16)
            for s in range(NSG):
                sp.dma_start(xs[:, s * SGT:(s + 1) * SGT, :], x_t[:, s * SGT:(s + 1) * SGT, :]).then_inc(x_in[s], 16)
                if s == 1:
                    sp.dma_start(w1f[:, :].rearrange("p (e h) -> p e h", e=E), w1.rearrange("e d h -> d e h")
                                 ).then_inc(w1_in, 16)
            sp.dma_start(w2f[:, :].rearrange("p (e c o) -> p e c o", e=E, c=HC),
                         w2.rearrange("e (c p) o -> p e c o", p=P)).then_inc(w2_in, 16)
            sp.wait_ge(setup_dve, 5)
            sp.dma_start(mod_rows, modr[:, :, :].rearrange("b m d -> b (m d)")).then_inc(modrow_out, 16)
            sp.wait_ge(modrow_out, 16)
            with sp.Fori(0, NSG) as sg:
                for q in range(NQ):
                    sp.wait_ge(h2_ready, sg * NQ)
                    src = mod_rows[bass.ds(sg * (NQ * GB) + q * GB, GB), 0:2 * D]
                    sp.dma_start(mb[q][:, :, :, :].rearrange("p b m d -> p b (m d)"),
                                 src.partition_broadcast(P)).then_inc(mb_in[q], 16)
            sp.wait_ge(table_ready, 1)
            padv = padt[:, :, :].rearrange("p t r -> p (t r)")
            with sp.Fori(0, PAIRS) as j:
                row = sp.value_load(padrow[0:1, bass.ds(j, 1)], min_val=0, max_val=ROWS - TW)
                sp.dma_start(sorted_rows[bass.ds(row, TW), :].rearrange("(p t) r -> p (t r)", p=P), padv
                             ).then_inc(pad_out, 16)
            sp.dma_start(sorted_rows[PAIRS * STRIDE:ROWS, :].rearrange("(p t) r -> p (t r)", p=P), padv
                         ).then_inc(pad_out, 16)
            sp.wait_ge(pad_out, 16 * (PAIRS + 1))
            for q in range(NQ):
                sp.wait_ge(scattered[q], 16 * GT * NSG)

            def load_tile(it, k):
                row = sp.value_load(table[0:1, bass.ds(it * BUFS + k, 1)], min_val=0, max_val=ROWS - TW)
                sp.dma_start(xin[k][:, :, :], sorted_rows[bass.ds(row, TW), :].rearrange("(t p) r -> p t r", p=P)
                             ).then_inc(tile_in[k], 16)

            turns = loop_turns(sp)
            for k in range(BUFS):
                load_tile(0, k)
            with sp.Fori(1, turns) as it:
                for k in range(BUFS):
                    sp.wait_ge(xl_ready, it * (2 * BUFS) + (2 * (k - BUFS) + 2))
                    sp.sem_inc(sp_turn, 1)
                    load_tile(it, k)
            sp.wait_ge(xl_ready, last_turn(sp) * (2 * BUFS) + 2)
            sp.sem_inc(sp_turn, 1)
            load_tile(turns, 0)
            for k in range(BUFS):
                sp.wait_ge(ysc[k], turns * (16 * HALVES))
                sp.sem_inc(sp_turn, 1)
            with sp.Fori(0, NSG) as sg:
                for q in range(NQ):
                    g = sg * NQ + q
                    sp.wait_ge(yout_ready, sg * NQ)
                    sp.dma_start(yin[q][:, :, :], moe_t[:, bass.ds(sg * SGT + q * GT, GT), :]).then_inc(yin_done[q], 16)
                    sp.dma_start(gin[q][:, :, :],
                                 mod_rows[bass.ds(sg * (NQ * GB) + q * GB, GB), 2 * D:3 * D].partition_broadcast(P)
                                 ).then_inc(yin_done[q], 16)

        @block.gpsimd
        def _(pool):
            done = 0

            def mark(ins):
                nonlocal done
                done += 1
                ins.then_inc(pool_step, 1)

            def join():
                pool.wait_ge(pool_step, done)

            for t in (ones16, ones_bf, onesf, upper):
                mark(pool.memset(t[:, :], 1.0))
            for t in (ident, b2row, seen):
                mark(pool.memset(t[:, :], 0.0))
            mark(pool.memset(padt[:, :, :], 0.0))
            mark(pool.memset(eps_col[:, :], EPS))
            mark(pool.memset(pay[:, :, D:ROW], 0.0))
            mark(pool.iota(tok[:, :], pattern=[[P, NT]], base=0, channel_multiplier=1))
            mark(pool.iota(cntt[:, :], pattern=[[1, PAIRS]], base=0, channel_multiplier=0))
            mark(pool.iota(cnti[:, 0:1], pattern=[[0, 1]], base=0, channel_multiplier=1))
            mark(pool.iota(cnti[:, E:2 * E], pattern=[[-1, E]], base=E, channel_multiplier=0))
            join()
            mark(pool.memset(padt[:, :, D + 2:D + 3].bitcast(I32), NOTOK))
            mark(pool.affine_select(out=ident[:, :], in_=ident[:, :], compare_op=ALU.not_equal, fill=1.0, base=0,
                                    pattern=[[-1, P]], channel_multiplier=1))
            mark(pool.affine_select(out=upper[:, :], in_=upper[:, :], compare_op=ALU.is_gt, fill=0.0, base=0,
                                    pattern=[[1, P]], channel_multiplier=-1))
            mark(pool.tensor_copy(pair_iota[:, :], cntt[:, :]))
            mark(pool.tensor_copy(pidx[:, :], cnti[:, 0:1]))
            mark(pool.tensor_copy(desc[:, :], cnti[:, E:2 * E]))
            join()
            mark(pool.tensor_scalar(region0[:, :], pair_iota[:, :], float(STRIDE), None, ALU.mult))
            for hi in range(1, E):
                first = hi * (hi - 1) // 2
                mark(pool.memset(ehi_of[:, first:first + hi], float(hi * H)))
                mark(pool.tensor_scalar(elo_of[:, first:first + hi], pair_iota[:, first:first + hi], float(first),
                                        float(H), ALU.subtract, ALU.mult))
            join()
            pool.memset(cnti[:, 0:1], 0).then_inc(iota_done, 1)
            for n, (f, hi, lo) in enumerate(((w1f, w1hi, w1lo), (w2f, w2hi, w2lo))):
                pool.wait_ge(w_hi, n + 1)
                pool.tensor_tensor(lo[:, :], f[:, :], hi[:, :], ALU.subtract).then_inc(w_lo, 1)

            with pool.Fori(0, NSG) as sg:
                for q in range(NQ):
                    pv = pay[:, q * GT:(q + 1) * GT, 0:D].rearrange("p (b t) d -> p b t d", b=GB)
                    pool.wait_ge(xn2_ready, sg * NQ + q + 1)
                    pool.wait_ge(mb_in[q], sg * 16 + 16)
                    pool.sem_inc(pool_turn, 1)

                    def row(m):
                        return mb[q][:, :, m, :].unsqueeze(2).to_broadcast([P, GB, GT // GB, D])
                    pool.tensor_tensor(pv, pv, row(1), ALU.mult).then_inc(pool_step, 1)
                    pool.wait_ge(pool_step, sg * NQ + q + 1 + done)
                    pool.sem_inc(pool_turn, 1)
                    pool.tensor_tensor(pv, pv, row(0), ALU.add).then_inc(h2_ready, 1)
                pool.wait_ge(idx_ready, sg + 1)
                pool.sem_inc(pool_turn, 1)
                for j in range(SGT):
                    pool.indirect_dma_start(sorted_rows, bass.IndirectOffsetOnAxis(idx[:, j:j + 1], 0),
                                            pay[:, j, :], None).then_inc(scattered[j // GT], 16)

            def scatter_tile(it, k):
                pool.wait_ge(ysb_ready, it * BUFS + (k + 1))
                pool.sem_inc(pool_turn, 1)
                for t in range(HALVES):
                    pool.indirect_dma_start(moe_rows, bass.IndirectOffsetOnAxis(meta[k][:, t, 2:3].bitcast(I32), 0),
                                            ysb[k][:, t, :], None, bounds_check=TOK - 1, oob_is_err=False
                                            ).then_inc(ysc[k], 16)

            pool.wait_ge(table_ready, 1)
            with pool.Fori(0, loop_turns(pool)) as it:
                for k in range(BUFS):
                    scatter_tile(it, k)
            with pool.Fori(0, NSG) as sg:
                for q in range(NQ):
                    pool.wait_ge(yin_done[q], sg * 32 + 32)
                    pool.sem_inc(pool_turn, 1)
                    yv = yin[q][:, :, :].rearrange("p (b t) d -> p b t d", b=GB)
                    pool.tensor_tensor(yv, yv, gin[q][:, :, :].unsqueeze(2).to_broadcast([P, GB, GT // GB, D]),
                                       ALU.mult).then_inc(ymul_ready, 1)

        @block.scalar
        def _(act):
            act.wait_ge(consts_in, 16 * N_CONST)
            act.activation(ctanh[:, :], csb[:, :], ACT.Tanh, scale=0.5).then_inc(setup_act, 1)
            act.wait_ge(v1_ready, 1)
            act.wait_ge(iota_done, 1)
            act.activation(std1[:, :], lnt[:, 3, :], ACT.Sqrt, bias=eps_col[:, 0:1], scale=1.0 / D
                           ).then_inc(std1_ready, 1)
            for n, (arrived, f, hi) in enumerate(((w1_in, w1f, w1hi), (w2_in, w2f, w2hi))):
                act.wait_ge(arrived, 16)
                act.activation(hi[:, :], f[:, :], ACT.Copy).then_inc(w_hi, 1)
            act.wait_ge(setup_dve, 5)

            with act.Fori(0, NSG) as sg:
                for q in range(NQ):
                    g = sg * NQ + q
                    act.wait_ge(xnT_ready, g + 1)
                    act.wait_ge(z_ready, g)
                    for b in range(GB):
                        bb = g * GB + b
                        ins = act.activation(hT[:, b * S:(b + 1) * S], bank[0][:, b * S:(b + 1) * S], ACT.Identity,
                                             bias=sa[:, bass.ds(bb, 1)], scale=ca1[:, bass.ds(bb, 1)])
                    ins.then_inc(hT_ready, 1)
                    act.wait_ge(z_ready, g + 1)
                    act.wait_ge(r_ready, g)
                    act.activation(a[:, :], bank[2][:, :], ACT.Tanh, bias=bhalf[:, 1:2], scale=0.5
                                   ).then_inc(act_step, 1)
                    for b in range(GB):
                        bb = g * GB + b
                        act.activation(vs[:, b * S:(b + 1) * S], bank[3][:, b * S:(b + 1) * S], ACT.Identity,
                                       bias=gabv[:, bass.ds(bb, 1)], scale=gaN[:, bass.ds(bb, 1)])
                    act.activation(tg[:, :], bank[1][:, :], ACT.Tanh, bias=bhalf[:, 0:1], scale=0.5
                                   ).then_inc(z_used, 1)
                    act.wait_ge(act_step, g + 1)
                    act.activation(a[:, :], a[:, :], ACT.Copy, bias=0.5, scale=0.5).then_inc(gates_ready, 1)
                act.wait_ge(v2_ready, sg + 1)
                act.activation(std2[:, :], lnt[:, 3, 0:SGT], ACT.Sqrt, bias=eps_col[:, 0:1], scale=1.0 / D
                               ).then_inc(std2_ready, 1)
                for q in range(NQ):
                    g = sg * NQ + q
                    act.wait_ge(h2Tp_ready, g + 1)
                    act.wait_ge(lg_ready, g)
                    act.activation(h2T[:, :], bank[5][:, :], ACT.Copy).then_inc(h2T_ready, 1)
                act.wait_ge(d_ready, sg + 1)
                act.activation(Ex[:, :, :], L[:, :, :], ACT.Exp)
                act.activation(small["em2"][:, :], small["m2"][:, :], ACT.Exp).then_inc(e_ready, 1)

            def x_high(it, n):
                act.wait_ge(xT_ready, it * BUFS + (n + 1))
                if not (isinstance(it, int) and n < 2):
                    act.wait_ge(hps_ready, it * (2 * BUFS) + (2 * n - 2))
                act.activation(xh[n % 2][:, :], bank[4 + n % 2][:, 0:TW], ACT.Copy).then_inc(xh_ready, 1)

            def hidden(it, n):
                for e in range(2):
                    act.wait_ge(hps_ready, it * (2 * BUFS) + (2 * n + e + 1))
                    if e == 0:
                        act.wait_ge(bcols_ready, it * BUFS + (n + 1))
                    if not (isinstance(it, int) and n < 1):
                        act.wait_ge(hl_ready, it * (2 * BUFS) + (2 * n - 1 + e))
                    for cc in range(HC):
                        ins = act.activation(hf[e][:, cc, :], bank[2 * e + cc // 2][:, (cc % 2) * TW:(cc % 2 + 1) * TW],
                                             ACT.Relu, bias=bcols[n % 2][:, e * HC + cc:e * HC + cc + 1])
                    ins.then_inc(hf_ready, 1)

            def y_low(it, n):
                act.wait_ge(yps_ready, it * BUFS + (n + 1))
                if not (isinstance(it, int) and n < 1):
                    act.wait_ge(ysb_ready, it * BUFS + n)
                for t in range(HALVES):
                    ins = act.activation(ylo[:, t, :], bank[6 + t][:, 0:D], ACT.Copy, scale=meta[n % BUFS][:, t, 0:1])
                ins.then_inc(ylo_ready, 1)

            act.wait_ge(table_ready, 1)
            turns = loop_turns(act)
            x_high(0, 0)
            for n in range(BUFS):
                x_high(0, n + 1)
                hidden(0, n)
                if n:
                    y_low(0, n - 1)
            with act.Fori(1, turns) as it:
                for k in range(BUFS):
                    x_high(it, k + 1)
                    hidden(it, k)
                    y_low(it, k - 1)
            y_low(last_turn(act), BUFS - 1)
            with act.Fori(0, NSG) as sg:
                for q in range(NQ):
                    act.wait_ge(yout_ready, sg * NQ + q + 1)
                    act.dma_start(out_t[:, bass.ds(sg * SGT + q * GT, GT), :], yout[q][:, :, :]).then_inc(stored[q], 16)
            for q in range(NQ):
                act.wait_ge(stored[q], 16 * NSG)

        @block.vector
        def _(dve):
            base, steps = 0, 0

            def mark(ins):
                nonlocal steps
                ins.then_inc(dve_step, 1)
                steps += 1

            def join():
                dve.wait_ge(dve_step, base + steps)

            def step(ins):
                mark(ins)
                join()

            def signed_clamp(dst, sg_t, ab_t, src):
                step(dve.tensor_copy(dst, src))
                mark(dve.tensor_scalar(sg_t, dst, 0.0, 2.0, ALU.is_ge, ALU.mult))
                step(dve.tensor_scalar(ab_t, dst, -1.0, 0.25, ALU.mult, ALU.max))
                step(dve.tensor_tensor(ab_t, ab_t, dst, ALU.max))
                return dve.scalar_tensor_tensor(out=dst, in0=sg_t, scalar=1.0, in1=ab_t, op0=ALU.subtract, op1=ALU.mult)

            def variances(st, n):
                m0, M0, m1, M1 = (st[:, 0:n, i] for i in (1, 2, 4, 5))
                mark(dve.tensor_tensor(lnt[:, 0, 0:n], m0, m1, ALU.add))
                mark(dve.tensor_tensor(lnt[:, 1, 0:n], m0, m1, ALU.subtract))
                step(dve.tensor_tensor(lnt[:, 2, 0:n], M0, M1, ALU.add))
                step(dve.tensor_tensor(lnt[:, 1, 0:n], lnt[:, 1, 0:n], lnt[:, 1, 0:n], ALU.mult))
                return dve.scalar_tensor_tensor(out=lnt[:, 3, 0:n], in0=lnt[:, 1, 0:n], scalar=D / 4.0,
                                                in1=lnt[:, 2, 0:n], op0=ALU.mult, op1=ALU.add)

            def scales(std, rstd, nmr, n):
                step(dve.reciprocal(rstd[:, 0:n], std[:, 0:n]))
                step(dve.scalar_tensor_tensor(out=nmr[:, 0:n], in0=lnt[:, 0, 0:n], scalar=-0.5, in1=rstd[:, 0:n],
                                              op0=ALU.mult, op1=ALU.mult))

            dve.wait_ge(consts_in, 16 * N_CONST)
            dve.wait_ge(iota_done, 1)
            mark(dve.tensor_scalar(bhalf[:, :], bcol[:, 0:2], 0.5, None, ALU.mult))
            dve.wait_ge(setup_act, 1)
            step(dve.scalar_tensor_tensor(out=csilu[:, :], in0=ctanh[:, :], scalar=1.0, in1=csb[:, :],
                                          op0=ALU.add, op1=ALU.mult))
            dve.tensor_scalar(csilu[:, :], csilu[:, :], 0.5, None, ALU.mult).then_inc(setup_dve, 1)
            dve.wait_ge(setup_pe, 1)
            dve.tensor_copy(csT[:, :], bank[0][:, 0:B]).then_inc(setup_dve, 1)
            dve.wait_ge(setup_pe, 2)
            dve.tensor_copy(wT[:, :, :], bank[1][:, 0:3 * D].rearrange("p (m d) -> p m d", m=3))
            mark(dve.tensor_copy(b1col[:, :], bank[2][:, 2 * E:2 * E + E * HC]))
            dve.tensor_copy(gwT[:, :], bank[2][:, 0:E]).then_inc(setup_dve, 1)
            dve.wait_ge(setup_pe, 3)
            mark(dve.tensor_copy(sa[:, :], bank[3][:, 0:B]))
            mark(dve.tensor_scalar(ca1[:, :], bank[3][:, B:2 * B], 1.0, None, ALU.add))
            step(signed_clamp(gaN[:, :], gasg[:, :], gaab[:, :], bank[3][:, 2 * B:3 * B]))
            step(dve.tensor_scalar(gaN[:, :], gaN[:, :], -0.5, None, ALU.mult))
            dve.tensor_scalar(gabv[:, :], gaN[:, :], bcol[:, 2:3], None, ALU.mult).then_inc(setup_dve, 1)
            dve.tensor_copy(modr[:, 0, :], bank[4][0:B, 0:D])
            dve.tensor_scalar(modr[:, 1, :], bank[4][0:B, D:2 * D], 1.0, None, ALU.add)
            signed_clamp(modr[:, 2, :], gbsg[:, :], gbab[:, :], bank[4][0:B, 2 * D:3 * D]).then_inc(setup_dve, 1)
            b2v = [b2row[r:r + 1, :].rearrange("p (e h) -> p e h", e=E)[:, :, 0:D] for r in (0, 32)]
            b2f = bstage[:, :].rearrange("p (e d) -> p e d", e=E)
            step(dve.tensor_copy(b2v[0], b2f))
            mark(dve.tensor_tensor(b2v[1], b2f, b2v[0], ALU.subtract))
            for s in range(NSG):
                dve.wait_ge(x_in[s], 16)
                with dve.Fori(0, SGT // GT) as t4:
                    for k in range(GT):
                        t = t4 * GT + (s * SGT + k)
                        dve.bn_stats(st1[:, bass.ds(t, 1), :].rearrange("p o s -> p (o s)"),
                                     xs[:, bass.ds(t, 1), :].rearrange("p o d -> p (o d)")).then_inc(dve_step, 1)
                steps += SGT
            join()
            variances(st1, NT).then_inc(v1_ready, 1)
            dve.wait_ge(std1_ready, 1)
            scales(std1, rstd1, nmr1, NT)

            start, steps = steps, 0
            steps_per_sg = 50
            m = {n: t[:, :] for n, t in small.items()}

            def wide(t2, n):
                return t2.unsqueeze(2).to_broadcast([P, SGT, n])

            def over_tiles(t2, n):
                return t2.unsqueeze(1).to_broadcast([P, SGT, n])

            with dve.Fori(0, NSG) as sg:
                base = sg * steps_per_sg + start

                def normalize(q):
                    dve.wait_ge(xnT_ready, sg * NQ + q)
                    for j in range(GT):
                        t = sg * SGT + (q * GT + j)
                        ins = dve.tensor_scalar(xn[:, j * P:(j + 1) * P],
                                                xs[:, bass.ds(t, 1), :].rearrange("p o d -> p (o d)"),
                                                rstd1[:, bass.ds(t, 1)], nmr1[:, bass.ds(t, 1)], ALU.mult, ALU.add)
                    ins.then_inc(xn_ready, 1)

                normalize(0)
                for q in range(NQ):
                    g = sg * NQ + q
                    if q + 1 < NQ:
                        normalize(q + 1)
                    dve.wait_ge(gates_ready, g + 1)
                    step(dve.scalar_tensor_tensor(out=u[:, :], in0=a[:, :], scalar=1.0, in1=vs[:, :],
                                                  op0=ALU.subtract, op1=ALU.mult))
                    for b in range(GB):
                        half = slice(b * S, (b + 1) * S)
                        mark(dve.tensor_tensor_scan(hs[:, half], a[:, half], u[:, half], 0.0, ALU.mult, ALU.add))
                    join()
                    dve.wait_ge(rT_ready, g)
                    dve.scalar_tensor_tensor(out=r[:, :], in0=tg[:, :], scalar=1.0, in1=hs[:, :],
                                             op0=ALU.add, op1=ALU.mult).then_inc(r_ready, 1)
                    dve.wait_ge(rT_ready, g + 1)
                    xg = xs[:, bass.ds(sg * SGT + q * GT, GT), :]
                    dve.tensor_tensor(xg, bank[4][:, :].rearrange("p (t d) -> p t d", t=GT), xg,
                                      ALU.add).then_inc(x1_ready, 1)
                    dve.wait_ge(x1_ready, g + 1)
                    dve.sem_inc(dve_turn, 1)
                    for j in range(GT):
                        t = sg * SGT + (q * GT + j)
                        ins = dve.bn_stats(st2[:, q * GT + j, :], xs[:, bass.ds(t, 1), :].rearrange("p o d -> p (o d)"))
                step(ins)
                variances(st2, SGT).then_inc(v2_ready, 1)
                dve.wait_ge(std2_ready, sg + 1)
                scales(std2, rstd2, nmr2, SGT)
                for q in range(NQ):
                    dve.wait_ge(scattered[q], sg * (16 * GT))
                    for j in range(q * GT, (q + 1) * GT):
                        ins = dve.tensor_scalar(pay[:, j, 0:D],
                                                xs[:, bass.ds(sg * SGT + j, 1), :].rearrange("p o d -> p (o d)"),
                                                rstd2[:, j:j + 1], nmr2[:, j:j + 1], ALU.mult, ALU.add)
                    ins.then_inc(xn2_ready, 1)
                dve.wait_ge(lg_ready, sg * NQ + NQ)
                dve.tensor_tensor(L[:, :, :], bank[6][:, 0:SGT * E].rearrange("p (t e) -> p t e", e=E),
                                  over_tiles(gbias[:, :], E), ALU.add).then_inc(L_ready, 1)
                dve.wait_ge(L_ready, sg + 1)
                step(dve.tensor_reduce(m["m1"], L[:, :, :], AX_X, ALU.max))
                step(dve.tensor_tensor(L[:, :, :], L[:, :, :], wide(m["m1"], E), ALU.subtract))
                step(dve.scalar_tensor_tensor(out=cand[:, :, :], in0=L[:, :, :], scalar=0.0,
                                              in1=over_tiles(desc[:, :], E), op0=ALU.is_equal, op1=ALU.mult))
                step(dve.tensor_reduce(m["c1"], cand[:, :, :], AX_X, ALU.max))
                step(dve.tensor_tensor(oh1[:, :, :], over_tiles(desc[:, :], E), wide(m["c1"], E), ALU.is_equal))
                step(dve.scalar_tensor_tensor(out=D2[:, :, :], in0=oh1[:, :, :], scalar=NEG, in1=L[:, :, :],
                                              op0=ALU.mult, op1=ALU.add))
                dve.tensor_reduce(m["m2"], D2[:, :, :], AX_X, ALU.max).then_inc(d_ready, 1)
                dve.wait_ge(d_ready, sg + 1)
                step(dve.tensor_tensor(cand[:, :, :], D2[:, :, :], wide(m["m2"], E), ALU.is_equal))
                step(dve.tensor_tensor(cand[:, :, :], cand[:, :, :], over_tiles(desc[:, :], E), ALU.mult))
                step(dve.tensor_reduce(m["c2"], cand[:, :, :], AX_X, ALU.max))
                mark(dve.tensor_tensor(m["cmax"], m["c1"], m["c2"], ALU.max))
                mark(dve.tensor_tensor(m["cmin"], m["c1"], m["c2"], ALU.min))
                mark(dve.tensor_tensor(m["isl"], m["c1"], m["c2"], ALU.is_gt))
                step(dve.tensor_tensor(m["ish"], m["c1"], m["c2"], ALU.is_lt))
                mark(dve.tensor_scalar(m["elo"], m["cmax"], -1.0, float(E), ALU.mult, ALU.add))
                step(dve.tensor_scalar(m["ehi"], m["cmin"], -1.0, float(E), ALU.mult, ALU.add))
                step(dve.scalar_tensor_tensor(out=m["tri"], in0=m["ehi"], scalar=1.0, in1=m["ehi"],
                                              op0=ALU.subtract, op1=ALU.mult))
                step(dve.scalar_tensor_tensor(out=m["pair"], in0=m["tri"], scalar=0.5, in1=m["elo"],
                                              op0=ALU.mult, op1=ALU.add))
                dve.tensor_tensor(OH[:, :, :], over_tiles(pair_iota[:, :], PAIRS), wide(m["pair"], PAIRS),
                                  ALU.is_equal).then_inc(oh_ready, 1)
                dve.wait_ge(e_ready, sg + 1)
                step(dve.tensor_reduce(m["s"], Ex[:, :, :], AX_X, ALU.add))
                step(dve.reciprocal(m["p1"], m["s"]))
                step(dve.tensor_tensor(m["p2"], m["em2"], m["p1"], ALU.mult))
                mark(dve.tensor_tensor(m["t1"], m["isl"], m["p1"], ALU.mult))
                mark(dve.tensor_tensor(m["t2"], m["ish"], m["p2"], ALU.mult))
                mark(dve.tensor_tensor(m["t3"], m["ish"], m["p1"], ALU.mult))
                step(dve.tensor_tensor(m["t4"], m["isl"], m["p2"], ALU.mult))
                mark(dve.tensor_tensor(pay[:, :, D], m["t1"], m["t2"], ALU.add))
                mark(dve.tensor_tensor(pay[:, :, D + 1], m["t3"], m["t4"], ALU.add))
                mark(dve.tensor_copy(payi[:, :, D + 2], tok[:, bass.ds(sg * SGT, SGT)]))
                dve.wait_ge(oh_ready, sg + 1)
                step(dve.tensor_reduce(seen_add[:, :], OH[:, :, :].rearrange("p t j -> p j t"), AX_X, ALU.add))
                dve.wait_ge(rank_ready, sg + 1)
                mark(dve.tensor_tensor(seen[:, :], seen[:, :], seen_add[:, :], ALU.add))
                step(dve.tensor_tensor(prod[:, :, :], bank[7][:, 0:SGT * PAIRS].rearrange("p (t j) -> p t j", j=PAIRS),
                                       OH[:, :, :], ALU.mult))
                step(dve.tensor_reduce(m["pos"], prod[:, :, :], AX_X, ALU.add))
                dve.scalar_tensor_tensor(out=idx[:, :], in0=m["pair"], scalar=float(STRIDE), in1=m["pos"],
                                         op0=ALU.mult, op1=ALU.add).then_inc(idx_ready, 1)
            assert steps == steps_per_sg, steps
            base, steps = start + NSG * steps_per_sg, 0
            dve.wait_ge(cnt_ready, 1)
            step(dve.tensor_copy(cnt[:, :], bank[6][:, 0:PAIRS]))
            mark(dve.tensor_tensor(padrow[:, :], cnt[0:1, :], region0[0:1, :], ALU.add))
            step(dve.tensor_scalar(cnti[:, :], cnt[:, :], float(TW - 1), None, ALU.add))
            step(dve.tensor_scalar(cntt[:, :], cnti[:, :], TW.bit_length() - 1, None, ALU.arith_shift_right))
            step(dve.tensor_copy(ntl[:, :], cntt[:, :]))
            step(dve.tensor_tensor_scan(tend[:, :], onesf[:, :], ntl[:, :], 0.0, ALU.mult, ALU.add))
            mark(dve.tensor_scalar(le_end[:, :], tend[:, :], pidx[:, 0:1], None, ALU.is_le))
            step(dve.tensor_tensor(tstart[:, :], tend[:, :], ntl[:, :], ALU.subtract))
            step(dve.tensor_scalar(le_start[:, :], tstart[:, :], pidx[:, 0:1], None, ALU.is_le))
            step(dve.tensor_tensor(inpair[:, :], le_start[:, :], le_end[:, :], ALU.subtract))
            mark(dve.scalar_tensor_tensor(out=tt[:, 0, :], in0=tstart[:, :], scalar=pidx[:, 0:1], in1=inpair[:, :],
                                          op0=ALU.subtract, op1=ALU.mult))
            mark(dve.tensor_tensor(tt[:, 1, :], inpair[:, :], elo_of[:, :], ALU.mult))
            step(dve.tensor_tensor(tt[:, 2, :], inpair[:, :], ehi_of[:, :], ALU.mult))
            mark(dve.tensor_reduce(ngone[:, :], le_end[:, :], AX_X, ALU.add))
            step(dve.tensor_scalar(cnti[:, 0:1], tend[:, PAIRS - 1:PAIRS], float(BUFS - 1), None, ALU.add))
            step(dve.tensor_scalar(cntt[:, 0:1], cnti[:, 0:1], 2, None, ALU.arith_shift_right))
            mark(dve.tensor_tensor(tcols[:, 3:4], cntt[:, 0:1], pidx[:, :], ALU.subtract))
            step(dve.tensor_reduce(tcols[:, 0:3], tt[:, :, :], AX_X, ALU.add))
            step(dve.tensor_scalar(base0[:, :], ngone[:, :], float(STRIDE), None, ALU.mult))
            dve.scalar_tensor_tensor(out=tcols[:, 0:1], in0=tcols[:, 0:1], scalar=-float(TW), in1=base0[:, :],
                                     op0=ALU.mult, op1=ALU.add).then_inc(tcols_ready, 1)
            dve.wait_ge(tcolsT_ready, 1)
            dve.tensor_copy(table[:, :], bank[6][0:4, 0:P]).then_inc(table_ready, 1)

            def x_low(it, n):
                k = n % BUFS
                dve.wait_ge(tile_in[k], it * 16 + (n // BUFS * 16 + 16))
                if not (isinstance(it, int) and n < BUFS):
                    dve.wait_ge(ysc[k], (it + n // BUFS) * (16 * HALVES))
                dve.tensor_copy(meta[k][:, :, :], xin[k][:, :, D:ROW]).then_inc(xl_ready, 1)
                dve.wait_ge(xh_ready, it * BUFS + (n + 1))
                dve.tensor_tensor(xl[n % 2][:, :], bank[4 + n % 2][:, 0:TW], xh[n % 2][:, :], ALU.subtract
                                  ).then_inc(xl_ready, 1)

            def biases(it, n):
                for e in range(2):
                    ex = dve.value_load(table[1 + e:2 + e, bass.ds(it * BUFS + n, 1)], min_val=0, max_val=(E - 1) * H)
                    ins = dve.tensor_copy(bcols[n % 2][:, e * HC:(e + 1) * HC], b1col[:, bass.ds(ex // P, HC)])
                ins.then_inc(bcols_ready, 1)

            def split(it, n):
                for e in range(2):
                    dve.wait_ge(hf_ready, it * (2 * BUFS) + (2 * n + e + 1))
                    if not (isinstance(it, int) and n < 2):
                        dve.wait_ge(yps_ready, it * BUFS + (n - 1))
                    dve.tensor_copy(hh[n % 2][e][:, :, :], hf[e][:, :, :]).then_inc(hh_ready, 1)
                    dve.wait_ge(hh_ready, it * (2 * BUFS) + (2 * n + e + 1))
                    dve.tensor_tensor(hl[n % 2][e][:, :, :], hf[e][:, :, :], hh[n % 2][e][:, :, :], ALU.subtract
                                      ).then_inc(hl_ready, 1)

            def y_sum(it, n):
                k = n % BUFS
                dve.wait_ge(ylo_ready, it * BUFS + (n + 1))
                for t in range(HALVES):
                    ins = dve.scalar_tensor_tensor(out=ysb[k][:, t, :], in0=bank[6 + t][:, D:2 * D],
                                                   scalar=meta[k][:, t, 1:2], in1=ylo[:, t, :],
                                                   op0=ALU.mult, op1=ALU.add)
                ins.then_inc(ysb_ready, 1)

            dve.wait_ge(table_ready, 1)
            turns = loop_turns(dve)
            biases(0, 0)
            x_low(0, 0)
            for n in range(BUFS):
                x_low(0, n + 1)
                biases(0, n + 1)
                split(0, n)
                if n:
                    y_sum(0, n - 1)
            with dve.Fori(1, turns) as it:
                for k in range(BUFS):
                    x_low(it, k + 1)
                    biases(it, k + 1)
                    split(it, k)
                    y_sum(it, k - 1)
            y_sum(last_turn(dve), BUFS - 1)
            with dve.Fori(0, NSG) as sg:
                for q in range(NQ):
                    dve.wait_ge(ymul_ready, sg * NQ + q + 1)
                    dve.wait_ge(stored[q], sg * 16)
                    dve.tensor_tensor(yout[q][:, :, :], yin[q][:, :, :], xs[:, bass.ds(sg * SGT + q * GT, GT), :],
                                      ALU.add).then_inc(yout_ready, 1)

        @block.tensor
        def _(pe):
            pe.wait_ge(consts_in, 16 * N_CONST)
            pe.wait_ge(iota_done, 1)
            pe.wait_ge(setup_dve, 1)
            pe.transpose(bank[0][:, 0:B], csilu[:, :], ident[0:B, 0:B]).then_inc(setup_pe, 1)
            for i in range(3):
                pe.transpose(bank[1][:, i * D:(i + 1) * D], wraw[:, i, :], ident[:, :])
            pe.transpose(bank[2][:, 2 * E:2 * E + E * HC], b1c[:, :], ident[0:E * HC, 0:E * HC])
            pe.transpose(bank[2][:, 0:E], gw[:, :], ident[0:E, 0:E]).then_inc(setup_pe, 1)
            pe.wait_ge(setup_dve, 2)
            for i in range(3):
                pe.matmul(bank[3][:, i * B:(i + 1) * B], wmods[:, i * D:(i + 1) * D], csT[:, :], start=True, stop=True)
            pe.matmul(bank[4][0:B, 0:3 * D], csT[:, :], wmods[:, 3 * D:6 * D], start=True, stop=True).then_inc(setup_pe, 1)
            pe.wait_ge(setup_dve, 3)

            with pe.Fori(0, NSG) as sg:
                for q in range(NQ):
                    g = sg * NQ + q
                    pe.wait_ge(xn_ready, g + 1)
                    pe.wait_ge(hT_ready, g)
                    for j in range(GT):
                        ins = pe.transpose(bank[0][:, j * P:(j + 1) * P], xn[:, j * P:(j + 1) * P], ident[:, :])
                    ins.then_inc(xnT_ready, 1)
                    pe.wait_ge(hT_ready, g + 1)
                    pe.wait_ge(z_used, g)
                    for i in (1, 2, 0):
                        ins = pe.matmul(bank[1 + i][:, :], wT[:, i, :], hT[:, :], start=True, stop=True)
                    ins.then_inc(z_ready, 1)
                    pe.wait_ge(r_ready, g + 1)
                    pe.wait_ge(x1_ready, g)
                    for j in range(GT):
                        ins = pe.transpose(bank[4][:, j * P:(j + 1) * P], r[:, j * P:(j + 1) * P], ident[:, :])
                    ins.then_inc(rT_ready, 1)
                pe.wait_ge(L_ready, sg)
                for q in range(NQ):
                    g = sg * NQ + q
                    pe.wait_ge(h2_ready, g + 1)
                    pe.wait_ge(h2T_ready, g)
                    for j in range(GT):
                        ins = pe.transpose(bank[5][:, j * P:(j + 1) * P], pay[:, q * GT + j, 0:D], ident[:, :])
                    ins.then_inc(h2Tp_ready, 1)
                    pe.wait_ge(h2T_ready, g + 1)
                    for j in range(GT):
                        o = (q * GT + j) * E
                        ins = pe.matmul(bank[6][:, o:o + E], h2T[:, j * P:(j + 1) * P], gwT[:, :], start=True, stop=True)
                    ins.then_inc(lg_ready, 1)
                pe.wait_ge(oh_ready, sg + 1)
                pe.wait_ge(idx_ready, sg)
                ohf = OH[:, :, :].rearrange("p t j -> p (t j)")
                rank = bank[7][:, 0:SGT * PAIRS]
                pe.matmul(rank, upper[:, :], ohf, start=True, stop=False)
                for t in range(1, SGT):
                    pe.matmul(rank[:, t * PAIRS:], ones_bf[:, :], ohf[:, 0:(SGT - t) * PAIRS], start=False, stop=False)
                pe.matmul(rank.rearrange("p (t j) -> p t j", j=PAIRS), ones_bf[:, :],
                          seen[:, :].unsqueeze(1).to_broadcast([P, SGT, PAIRS]), start=False, stop=True
                          ).then_inc(rank_ready, 1)
            pe.wait_ge(idx_ready, NSG)
            pe.matmul(bank[6][:, 0:PAIRS], ones_bf[:, :], seen[:, :], start=True, stop=True).then_inc(cnt_ready, 1)
            pe.wait_ge(tcols_ready, 1)
            pe.transpose(bank[6][0:4, 0:P], tcols[:, :], ident[:, :]).then_inc(tcolsT_ready, 1)
            pe.wait_ge(table_ready, 1)
            pe.wait_ge(w_lo, 2)

            def turn(it, n):
                pe.wait_ge(tile_in[n % BUFS], it * 16 + (n // BUFS * 16 + 16))
                for t in range(HALVES):
                    ins = pe.transpose(bank[4 + n % 2][:, t * P:(t + 1) * P], xin[n % BUFS][:, t, 0:D], ident[:, :])
                ins.then_inc(xT_ready, 1)

            def experts_of(it, n):
                return [pe.value_load(table[1 + e:2 + e, bass.ds(it * BUFS + n, 1)], min_val=0, max_val=(E - 1) * H)
                        for e in range(2)]

            def layer1(it, n, ex):
                pe.wait_ge(xl_ready, it * (2 * BUFS) + (2 * n + 2))
                for e in range(2):
                    if not (isinstance(it, int) and n < 1):
                        pe.wait_ge(hf_ready, it * (2 * BUFS) + (2 * n - 1 + e))
                    for cc in range(HC):
                        o = bank[2 * e + cc // 2][:, (cc % 2) * TW:(cc % 2 + 1) * TW]
                        whi, wlo = (w[:, bass.ds(ex[e] + cc * P, P)] for w in (w1hi, w1lo))
                        pe.matmul(o, whi, xh[n % 2][:, :], start=True, stop=False)
                        pe.matmul(o, whi, xl[n % 2][:, :], start=False, stop=False)
                        ins = pe.matmul(o, wlo, xh[n % 2][:, :], start=False, stop=True)
                    ins.then_inc(hps_ready, 1)

            def layer2(it, n, ex):
                if not (isinstance(it, int) and n < 1):
                    pe.wait_ge(ysb_ready, it * BUFS + n)
                pe.wait_ge(hl_ready, it * (2 * BUFS) + (2 * n + 2))
                for e in range(2):
                    o = [bank[6 + t][:, e * D:(e + 1) * D] for t in range(HALVES)]
                    bias = b2row[:, bass.ds(ex[e], D)]
                    for t in range(HALVES):
                        pe.matmul(o[t], ones16[:, :], bias, start=True, stop=False)
                    for cc in range(HC):
                        whi, wlo = (w[:, bass.ds(ex[e] + cc * D, D)] for w in (w2hi, w2lo))
                        for t in range(HALVES):
                            pe.matmul(o[t], hh[n % 2][e][:, cc, t * P:(t + 1) * P], whi, start=False, stop=False)
                            pe.matmul(o[t], hl[n % 2][e][:, cc, t * P:(t + 1) * P], whi, start=False, stop=False)
                        for t in range(HALVES):
                            ins = pe.matmul(o[t], hh[n % 2][e][:, cc, t * P:(t + 1) * P], wlo, start=False,
                                            stop=(cc == HC - 1))
                ins.then_inc(yps_ready, 1)

            turns = loop_turns(pe)
            turn(0, 0)
            for n in range(BUFS):
                now = experts_of(0, n)
                turn(0, n + 1)
                layer1(0, n, now)
                if n:
                    layer2(0, n - 1, before)
                before = now
            with pe.Fori(1, turns) as it:
                before = experts_of(it, -1)
                for k in range(BUFS):
                    now = experts_of(it, k)
                    turn(it, k + 1)
                    layer1(it, k, now)
                    layer2(it, k - 1, before)
                    before = now
            last = last_turn(pe)
            layer2(last, BUFS - 1, experts_of(last, BUFS - 1))


_INS = ["L0_attn_x", "L0_attn_Wg", "L0_attn_bg", "L0_attn_Wv", "L0_attn_bv", "L0_attn_Wd", "L0_attn_bd",
        "L0_ffn_gate_w", "L0_ffn_gate_b", "L0_ffn_w1", "L0_ffn_b1", "L0_ffn_w2", "L0_ffn_b2", "L0_c", "L0_wmod"]
_OUTS = [((B, S, D), "float32")]


def kernel(**inputs):
    import numpy as _np
    import concourse.bacc as _bacc
    from concourse import mybir as _mybir
    from concourse.bass_utils import run_bass_kernel_spmd as _run

    nc = _bacc.Bacc("TRN2", target_bir_lowering=False, num_devices=1)
    arrays, args = {}, []
    for name in _INS:
        arr = _np.ascontiguousarray(inputs[name])
        arrays[f"in_{name}_dram"] = arr
        args.append(nc.dram_tensor(f"in_{name}_dram", arr.shape, _mybir.dt.from_np(arr.dtype),
                                   kind="ExternalInput").ap())
    for i, (shape, dtype) in enumerate(_OUTS):
        dt = _mybir.dt.from_np(_np.dtype(dtype))
        args.append(nc.dram_tensor(f"out_{i}_dram", shape, dt, kind="ExternalOutput").ap())
    adaln_moe_kernel(nc, *args)
    res = _run(nc, [arrays], core_ids=[0])
    got = tuple(res.results[0][f"out_{i}_dram"] for i in range(len(_OUTS)))
    return got[0]
```

```python
from contextlib import ExitStack

import concourse.bass as bass
from concourse import mybir

ALU = mybir.AluOpType
ACT = mybir.ActivationFunctionType
F32 = mybir.dt.float32
F16 = mybir.dt.float16
BF16 = mybir.dt.bfloat16
I32 = mybir.dt.int32
AX_X = mybir.AxisListType.X

P = 128
B, S, D = 32, 256, 128
H, E = 512, 8
HC = H // P
TOK = B * S
NT = TOK // P
GT = 4
GW = GT * P
GB = GW // S
SGT = 16
NSG = NT // SGT
NQ = SGT // GT
PAIRS = E * (E - 1) // 2
TW = 256
HALVES = TW // P
STRIDE = TOK + TW
ROWS = PAIRS * STRIDE + TW
ROW = D + 4
NOTOK = 1 << 20
BUFS = 4
EPS = 1e-5
NEG = -1e30


def adaln_moe_kernel(nc, x, Wg, bg, Wv, bv, Wd, bd, gate_w, gate_b, w1, b1, w2, b2, c, wmod, out):
    x_t = x.rearrange("b (u p) d -> p (b u) d", p=P)
    out_t = out.rearrange("b (u p) d -> p (b u) d", p=P)
    sorted_rows = nc.dram_tensor("sorted_rows", (ROWS, ROW), F32).ap()
    moe_rows = nc.dram_tensor("moe_rows", (TOK, D), F32).ap()
    mod_rows = nc.dram_tensor("mod_rows", (B, 3 * D), F32).ap()
    moe_t = moe_rows.rearrange("(u p) d -> p u d", p=P)

    with ExitStack() as ctx:
        def sb(name, shape, dt=F32):
            return ctx.enter_context(nc.sbuf_tensor(name, shape, dt))

        def sem(name):
            return ctx.enter_context(nc.semaphore(name))

        bank = [ctx.enter_context(nc.psum_tensor(f"bank{i}", [P, 512], F32)) for i in range(8)]

        xs = sb("xs", [P, NT, D])
        w1hi = sb("w1hi", [P, E * H], F16)
        w1lo = sb("w1lo", [P, E * H], F16)
        w2hi = sb("w2hi", [P, E * H], F16)
        w2lo = sb("w2lo", [P, E * H], F16)
        b2row = sb("b2row", [P, E * H], F16)
        ones16 = sb("ones16", [P, P], F16)
        ident = sb("ident", [P, P])
        w1f = sb("w1f", [P, E * H])
        w2f = sb("w2f", [P, E * H])
        bstage = sb("bstage", [1, E * D])
        wraw = sb("wraw", [P, 3, D])
        wT = sb("wT", [P, 3, D])
        bcol = sb("bcol", [P, 3])
        bhalf = sb("bhalf", [P, 2])
        gw = sb("gw", [E, D])
        gwT = sb("gwT", [P, E])
        gbias = sb("gbias", [P, E])
        csb = sb("csb", [B, D])
        ctanh = sb("ctanh", [B, D])
        csilu = sb("csilu", [B, D])
        csT = sb("csT", [P, B])
        wmods = sb("wmods", [P, 6 * D])
        sa = sb("sa", [P, B])
        ca1 = sb("ca1", [P, B])
        gasg = sb("gasg", [P, B])
        gaab = sb("gaab", [P, B])
        gaN = sb("gaN", [P, B])
        gabv = sb("gabv", [P, B])
        modr = sb("modr", [B, 3, D])
        gbsg = sb("gbsg", [B, D])
        gbab = sb("gbab", [B, D])
        eps_col = sb("eps_col", [P, 1])
        st1 = sb("st1", [P, NT, 6])
        std1 = sb("std1", [P, NT])
        rstd1 = sb("rstd1", [P, NT])
        nmr1 = sb("nmr1", [P, NT])
        lnt = sb("lnt", [P, 4, NT])
        xn = [sb(f"xn{k}", [P, GW]) for k in range(2)]
        hT = [sb(f"hT{k}", [P, GW]) for k in range(2)]
        a = [sb(f"a{k}", [P, GW]) for k in range(2)]
        tg = [sb(f"tg{k}", [P, GW]) for k in range(2)]
        vs = [sb(f"vs{k}", [P, GW]) for k in range(2)]
        u = sb("u", [P, GW])
        hs = sb("hs", [P, GW])
        r = [sb(f"r{k}", [P, GW]) for k in range(2)]
        st2 = sb("st2", [P, SGT, 6])
        std2 = sb("std2", [P, SGT])
        rstd2 = sb("rstd2", [P, SGT])
        nmr2 = sb("nmr2", [P, SGT])
        pay = sb("pay", [P, SGT, ROW])
        payi = pay[:, :, :].bitcast(I32)
        mb = [sb(f"mb{q}", [P, GB, 2, D]) for q in range(NQ)]
        h2T = sb("h2T", [P, GW])
        L = sb("L", [P, SGT, E])
        Ex = sb("Ex", [P, SGT, E])
        cand = sb("cand", [P, SGT, E])
        oh1 = sb("oh1", [P, SGT, E])
        D2 = sb("D2", [P, SGT, E])
        desc = sb("desc", [P, E])
        small = {n: sb("r_" + n, [P, SGT]) for n in
                 ("m1", "m2", "c1", "c2", "s", "p1", "em2", "p2", "cmax", "cmin", "ehi", "elo", "tri",
                  "pair", "isl", "ish", "t1", "t2", "t3", "t4", "pos")}
        pair_iota = sb("pair_iota", [P, PAIRS])
        OH = sb("OH", [P, SGT, PAIRS], BF16)
        prod = sb("prod", [P, SGT, PAIRS])
        upper = sb("upper", [P, P], BF16)
        ones_bf = sb("ones_bf", [P, P], BF16)
        seen = sb("seen", [P, PAIRS], BF16)
        seen_add = sb("seen_add", [P, PAIRS])
        idx = sb("idx", [P, SGT], I32)
        tok = sb("tok", [P, NT], I32)
        cnt = sb("cnt", [P, PAIRS])
        cnti = sb("cnti", [P, PAIRS], I32)
        cntt = sb("cntt", [P, PAIRS], I32)
        ntl = sb("ntl", [P, PAIRS])
        tend = sb("tend", [P, PAIRS])
        tstart = sb("tstart", [P, PAIRS])
        onesf = sb("onesf", [P, PAIRS])
        le_end = sb("le_end", [P, PAIRS])
        le_start = sb("le_start", [P, PAIRS])
        inpair = sb("inpair", [P, PAIRS])
        tt = sb("tt", [P, 3, PAIRS])
        elo_of = sb("elo_of", [P, PAIRS])
        ehi_of = sb("ehi_of", [P, PAIRS])
        pidx = sb("pidx", [P, 1])
        negin = sb("negin", [P, 1])
        ngone = sb("ngone", [P, 1])
        base0 = sb("base0", [P, 1])
        tcols = sb("tcols", [P, 4])
        table = sb("table", [4, P], I32)
        padrow = sb("padrow", [1, PAIRS], I32)
        region0 = sb("region0", [P, PAIRS])
        padt = sb("padt", [P, HALVES, ROW])
        xin = [sb(f"xin{k}", [P, HALVES, ROW]) for k in range(BUFS)]
        meta = [sb(f"meta{k}", [P, HALVES, 4]) for k in range(BUFS)]
        xh = [sb(f"xh{k}", [P, TW], F16) for k in range(2)]
        xl = [sb(f"xl{k}", [P, TW], F16) for k in range(2)]
        hh = [[sb(f"hh{k}{e}", [P, HC, TW], F16) for e in range(2)] for k in range(2)]
        hl = [[sb(f"hl{k}{e}", [P, HC, TW], F16) for e in range(2)] for k in range(2)]
        hf = [w2f[:, (e + 1) * HC * TW:(e + 2) * HC * TW].rearrange("p (c t) -> p c t", c=HC) for e in range(2)]
        ylo = sb("ylo", [P, HALVES, D])
        ysb = [w2f[:, 3 * HC * TW + k * HALVES * D:3 * HC * TW + (k + 1) * HALVES * D].rearrange("p (t d) -> p t d", t=HALVES)
               for k in range(BUFS)]
        b1c = sb("b1c", [E * HC, P])
        b1col = sb("b1col", [P, E * HC])
        bcols = [sb(f"bcols{k}", [P, 2 * HC]) for k in range(2)]
        yin = [w1f[:, q * GW:(q + 1) * GW].rearrange("p (t d) -> p t d", t=GT) for q in range(NQ)]
        yout = [w1f[:, (NQ + q) * GW:(NQ + q + 1) * GW].rearrange("p (t d) -> p t d", t=GT) for q in range(NQ)]
        gin = [w2f[:, q * GB * D:(q + 1) * GB * D].rearrange("p (b d) -> p b d", b=GB) for q in range(NQ)]

        consts_in = sem("consts_in")
        x_in = [sem(f"x_in{s}") for s in range(NSG)]
        w1_in, w2_in = sem("w1_in"), sem("w2_in")
        iota_done = sem("iota_done")
        dve_step, act_step, pool_step = sem("dve_step"), sem("act_step"), sem("pool_step")
        setup_pe, setup_dve, setup_act = sem("setup_pe"), sem("setup_dve"), sem("setup_act")
        w_hi, w_lo = sem("w_hi"), sem("w_lo")
        modrow_out = sem("modrow_out")
        v1_ready, std1_ready = sem("v1_ready"), sem("std1_ready")
        xn_ready, xnT_ready, hT_ready, z_ready = sem("xn_ready"), sem("xnT_ready"), sem("hT_ready"), sem("z_ready")
        z_used, gates_ready, r_ready, rT_ready, x1_ready = (sem("z_used"), sem("gates_ready"), sem("r_ready"),
                                                            sem("rT_ready"), sem("x1_ready"))
        v2_ready, std2_ready, xn2_ready, h2_ready = sem("v2_ready"), sem("std2_ready"), sem("xn2_ready"), sem("h2_ready")
        mb_in = [sem(f"mb_in{q}") for q in range(NQ)]
        h2Tp_ready, h2T_ready, lg_ready, L_ready = sem("h2Tp_ready"), sem("h2T_ready"), sem("lg_ready"), sem("L_ready")
        d_ready, e_ready, oh_ready, rank_ready, idx_ready = (sem("d_ready"), sem("e_ready"), sem("oh_ready"),
                                                             sem("rank_ready"), sem("idx_ready"))
        scattered = [sem(f"scattered{q}") for q in range(NQ)]
        cnt_ready, tcols_ready, tcolsT_ready, table_ready = (sem("cnt_ready"), sem("tcols_ready"),
                                                             sem("tcolsT_ready"), sem("table_ready"))
        pad_out = sem("pad_out")
        tile_in = [sem(f"tile_in{k}") for k in range(BUFS)]
        xT_ready, xh_ready, xl_ready = sem("xT_ready"), sem("xh_ready"), sem("xl_ready")
        hps_ready, hh_ready, hl_ready = sem("hps_ready"), sem("hh_ready"), sem("hl_ready")
        hf_ready, bcols_ready = sem("hf_ready"), sem("bcols_ready")
        yps_ready, ylo_ready, ysb_ready = sem("yps_ready"), sem("ylo_ready"), sem("ysb_ready")
        ysc = [sem(f"ysc{k}") for k in range(BUFS)]
        yin_done = [sem(f"yin_done{q}") for q in range(NQ)]
        ymul_ready, yout_ready = sem("ymul_ready"), sem("yout_ready")
        stored = [sem(f"stored{q}") for q in range(NQ)]

        pool_turn, dve_turn, sp_turn = sem("pool_turn"), sem("dve_turn"), sem("sp_turn")

        N_CONST = 12
        SETUP_IOTA = 1

        def after(eng, signal, count):
            if not (isinstance(count, int) and count <= 0):
                eng.wait_ge(signal, count)

        def loop_turns(eng):
            return eng.value_load(table[3:4, 0:1], min_val=TOK // TW // BUFS, max_val=(TOK // TW + PAIRS) // BUFS)

        def last_turn(eng):
            return eng.value_load(table[3:4, 1:2], min_val=TOK // TW // BUFS - 1,
                                  max_val=(TOK // TW + PAIRS) // BUFS - 1)

        block = ctx.enter_context(nc.Block())

        @block.sync
        def _(sp):
            for dst, src in ((csb[:], c), (wmods[:], wmod), (wraw[:, 0, :], Wg), (wraw[:, 1, :], Wd),
                             (wraw[:, 2, :], Wv), (gw[:], gate_w),
                             (bcol[:, 0:1], bg.rearrange("(p o) -> p o", o=1)),
                             (bcol[:, 1:2], bd.rearrange("(p o) -> p o", o=1)),
                             (bcol[:, 2:3], bv.rearrange("(p o) -> p o", o=1)),
                             (gbias[:], gate_b.partition_broadcast(P)),
                             (b1c[:, :], b1.rearrange("e (c p) -> (e c) p", p=P)),
                             (bstage[:, :], b2.rearrange("(o e) d -> o (e d)", o=1))):
                sp.dma_start(dst, src).then_inc(consts_in, 16)
            for s in range(NSG):
                sp.dma_start(xs[:, s * SGT:(s + 1) * SGT, :], x_t[:, s * SGT:(s + 1) * SGT, :]).then_inc(x_in[s], 16)
                if s == 1:
                    sp.dma_start(w1f[:, :].rearrange("p (e h) -> p e h", e=E), w1.rearrange("e d h -> d e h")
                                 ).then_inc(w1_in, 16)
            sp.dma_start(w2f[:, :].rearrange("p (e c o) -> p e c o", e=E, c=HC),
                         w2.rearrange("e (c p) o -> p e c o", p=P)).then_inc(w2_in, 16)
            sp.wait_ge(setup_dve, 5)
            sp.dma_start(mod_rows, modr[:, :, :].rearrange("b m d -> b (m d)")).then_inc(modrow_out, 16)
            sp.wait_ge(modrow_out, 16)
            def rows_for(sg):
                for q in range(NQ):
                    after(sp, h2_ready, sg * NQ)
                    src = mod_rows[bass.ds(sg * (NQ * GB) + q * GB, GB), 0:2 * D]
                    sp.dma_start(mb[q][:, :, :, :].rearrange("p b m d -> p b (m d)"),
                                 src.partition_broadcast(P)).then_inc(mb_in[q], 16)

            rows_for(0)
            with sp.Fori(1, NSG) as sg:
                rows_for(sg)
            sp.wait_ge(table_ready, 1)
            padv = padt[:, :, :].rearrange("p t r -> p (t r)")
            with sp.Fori(0, PAIRS) as j:
                row = sp.value_load(padrow[0:1, bass.ds(j, 1)], min_val=0, max_val=ROWS - TW)
                sp.dma_start(sorted_rows[bass.ds(row, TW), :].rearrange("(p t) r -> p (t r)", p=P), padv
                             ).then_inc(pad_out, 16)
            sp.dma_start(sorted_rows[PAIRS * STRIDE:ROWS, :].rearrange("(p t) r -> p (t r)", p=P), padv
                         ).then_inc(pad_out, 16)
            sp.wait_ge(pad_out, 16 * (PAIRS + 1))
            for q in range(NQ):
                sp.wait_ge(scattered[q], 16 * GT * NSG)

            def load_tile(it, k):
                row = sp.value_load(table[0:1, bass.ds(it * BUFS + k, 1)], min_val=0, max_val=ROWS - TW)
                sp.dma_start(xin[k][:, :, :], sorted_rows[bass.ds(row, TW), :].rearrange("(t p) r -> p t r", p=P)
                             ).then_inc(tile_in[k], 16)

            turns = loop_turns(sp)
            for k in range(BUFS):
                load_tile(0, k)
            with sp.Fori(1, turns) as it:
                for k in range(BUFS):
                    sp.wait_ge(xl_ready, it * (2 * BUFS) + (2 * (k - BUFS) + 2))
                    sp.sem_inc(sp_turn, 1)
                    load_tile(it, k)
            sp.wait_ge(xl_ready, last_turn(sp) * (2 * BUFS) + 2)
            sp.sem_inc(sp_turn, 1)
            load_tile(turns, 0)
            for k in range(BUFS):
                sp.wait_ge(ysc[k], turns * (16 * HALVES))
                sp.sem_inc(sp_turn, 1)
            def load_results(sg):
                for q in range(NQ):
                    g = sg * NQ + q
                    after(sp, yout_ready, sg * NQ + (q + 1 - NQ))
                    sp.dma_start(yin[q][:, :, :], moe_t[:, bass.ds(sg * SGT + q * GT, GT), :]).then_inc(yin_done[q], 16)
                    sp.dma_start(gin[q][:, :, :],
                                 mod_rows[bass.ds(sg * (NQ * GB) + q * GB, GB), 2 * D:3 * D].partition_broadcast(P)
                                 ).then_inc(yin_done[q], 16)

            load_results(0)
            with sp.Fori(1, NSG) as sg:
                load_results(sg)

        @block.gpsimd
        def _(pool):
            done = 0

            def mark(ins):
                nonlocal done
                done += 1
                ins.then_inc(pool_step, 1)

            def join():
                pool.wait_ge(pool_step, done)

            for t in (ones16, ones_bf, onesf, upper):
                mark(pool.memset(t[:, :], 1.0))
            for t in (ident, b2row, seen):
                mark(pool.memset(t[:, :], 0.0))
            mark(pool.memset(padt[:, :, :], 0.0))
            mark(pool.memset(eps_col[:, :], EPS))
            mark(pool.memset(pay[:, :, D:ROW], 0.0))
            mark(pool.iota(tok[:, :], pattern=[[P, NT]], base=0, channel_multiplier=1))
            mark(pool.iota(cntt[:, :], pattern=[[1, PAIRS]], base=0, channel_multiplier=0))
            mark(pool.iota(cnti[:, 0:1], pattern=[[0, 1]], base=0, channel_multiplier=1))
            mark(pool.iota(cnti[:, E:2 * E], pattern=[[-1, E]], base=E, channel_multiplier=0))
            join()
            mark(pool.memset(padt[:, :, D + 2:D + 3].bitcast(I32), NOTOK))
            mark(pool.affine_select(out=ident[:, :], in_=ident[:, :], compare_op=ALU.not_equal, fill=1.0, base=0,
                                    pattern=[[-1, P]], channel_multiplier=1))
            mark(pool.affine_select(out=upper[:, :], in_=upper[:, :], compare_op=ALU.is_gt, fill=0.0, base=0,
                                    pattern=[[1, P]], channel_multiplier=-1))
            mark(pool.tensor_copy(pair_iota[:, :], cntt[:, :]))
            mark(pool.tensor_copy(pidx[:, :], cnti[:, 0:1]))
            mark(pool.tensor_copy(desc[:, :], cnti[:, E:2 * E]))
            join()
            mark(pool.tensor_scalar(region0[:, :], pair_iota[:, :], float(STRIDE), None, ALU.mult))
            for hi in range(1, E):
                first = hi * (hi - 1) // 2
                mark(pool.memset(ehi_of[:, first:first + hi], float(hi * H)))
                mark(pool.tensor_scalar(elo_of[:, first:first + hi], pair_iota[:, first:first + hi], float(first),
                                        float(H), ALU.subtract, ALU.mult))
            join()
            pool.memset(cnti[:, 0:1], 0).then_inc(iota_done, 1)
            for n, (f, hi, lo) in enumerate(((w1f, w1hi, w1lo), (w2f, w2hi, w2lo))):
                pool.wait_ge(w_hi, n + 1)
                pool.tensor_tensor(lo[:, :], f[:, :], hi[:, :], ALU.subtract).then_inc(w_lo, 1)

            def sorted_group(sg):
                for q in range(NQ):
                    pv = pay[:, q * GT:(q + 1) * GT, 0:D].rearrange("p (b t) d -> p b t d", b=GB)
                    pool.wait_ge(xn2_ready, sg * NQ + q + 1)
                    pool.wait_ge(mb_in[q], sg * 16 + 16)
                    pool.sem_inc(pool_turn, 1)

                    def row(m):
                        return mb[q][:, :, m, :].unsqueeze(2).to_broadcast([P, GB, GT // GB, D])
                    pool.tensor_tensor(pv, pv, row(1), ALU.mult).then_inc(pool_step, 1)
                    pool.wait_ge(pool_step, sg * NQ + q + 1 + done)
                    pool.sem_inc(pool_turn, 1)
                    pool.tensor_tensor(pv, pv, row(0), ALU.add).then_inc(h2_ready, 1)
                pool.wait_ge(idx_ready, sg + 1)
                pool.sem_inc(pool_turn, 1)
                for j in range(SGT):
                    pool.indirect_dma_start(sorted_rows, bass.IndirectOffsetOnAxis(idx[:, j:j + 1], 0),
                                            pay[:, j, :], None).then_inc(scattered[j // GT], 16)

            sorted_group(0)
            with pool.Fori(1, NSG) as sg:
                sorted_group(sg)

            def scatter_tile(it, k):
                pool.wait_ge(ysb_ready, it * BUFS + (k + 1))
                pool.sem_inc(pool_turn, 1)
                for t in range(HALVES):
                    pool.indirect_dma_start(moe_rows, bass.IndirectOffsetOnAxis(meta[k][:, t, 2:3].bitcast(I32), 0),
                                            ysb[k][:, t, :], None, bounds_check=TOK - 1, oob_is_err=False
                                            ).then_inc(ysc[k], 16)

            pool.wait_ge(table_ready, 1)
            with pool.Fori(0, loop_turns(pool)) as it:
                for k in range(BUFS):
                    scatter_tile(it, k)
            def scale_group(sg):
                for q in range(NQ):
                    pool.wait_ge(yin_done[q], sg * 32 + 32)
                    pool.sem_inc(pool_turn, 1)
                    yv = yin[q][:, :, :].rearrange("p (b t) d -> p b t d", b=GB)
                    pool.tensor_tensor(yv, yv, gin[q][:, :, :].unsqueeze(2).to_broadcast([P, GB, GT // GB, D]),
                                       ALU.mult).then_inc(ymul_ready, 1)

            scale_group(0)
            with pool.Fori(1, NSG) as sg:
                scale_group(sg)

        @block.scalar
        def _(act):
            act.wait_ge(consts_in, 16 * N_CONST)
            act.activation(ctanh[:, :], csb[:, :], ACT.Tanh, scale=0.5).then_inc(setup_act, 1)
            act.wait_ge(v1_ready, 1)
            act.wait_ge(iota_done, 1)
            act.activation(std1[:, :], lnt[:, 3, :], ACT.Sqrt, bias=eps_col[:, 0:1], scale=1.0 / D
                           ).then_inc(std1_ready, 1)
            for n, (arrived, f, hi) in enumerate(((w1_in, w1f, w1hi), (w2_in, w2f, w2hi))):
                act.wait_ge(arrived, 16)
                act.activation(hi[:, :], f[:, :], ACT.Copy).then_inc(w_hi, 1)
            act.wait_ge(setup_dve, 5)

            def modulate(sg, q):
                g = sg * NQ + q
                act.wait_ge(xnT_ready, g + 1)
                after(act, z_ready, g - 1)
                for b in range(GB):
                    bb = g * GB + b
                    ins = act.activation(hT[q % 2][:, b * S:(b + 1) * S], bank[0][:, b * S:(b + 1) * S],
                                         ACT.Identity, bias=sa[:, bass.ds(bb, 1)], scale=ca1[:, bass.ds(bb, 1)])
                ins.then_inc(hT_ready, 1)

            def gates(sg, q):
                g = sg * NQ + q
                k = q % 2
                act.wait_ge(z_ready, g + 1)
                after(act, r_ready, g - 1)
                act.activation(a[k][:, :], bank[2][:, :], ACT.Tanh, bias=bhalf[:, 1:2], scale=0.5
                               ).then_inc(act_step, 1)
                for b in range(GB):
                    bb = g * GB + b
                    act.activation(vs[k][:, b * S:(b + 1) * S], bank[3][:, b * S:(b + 1) * S], ACT.Identity,
                                   bias=gabv[:, bass.ds(bb, 1)], scale=gaN[:, bass.ds(bb, 1)])
                act.activation(tg[k][:, :], bank[1][:, :], ACT.Tanh, bias=bhalf[:, 0:1], scale=0.5
                               ).then_inc(z_used, 1)
                act.wait_ge(act_step, g + 1)
                act.activation(a[k][:, :], a[k][:, :], ACT.Copy, bias=0.5, scale=0.5).then_inc(gates_ready, 1)

            def mixer(sg, last=False):
                for q in range(1, NQ):
                    if not (last and q + 1 == NQ):
                        modulate(sg, q + 1)
                    gates(sg, q)
                act.wait_ge(v2_ready, sg + 1)
                act.activation(std2[:, :], lnt[:, 3, 0:SGT], ACT.Sqrt, bias=eps_col[:, 0:1], scale=1.0 / D
                               ).then_inc(std2_ready, 1)
                if not last:
                    modulate(sg, NQ + 1)
                    gates(sg, NQ)
                for q in range(NQ):
                    g = sg * NQ + q
                    act.wait_ge(h2Tp_ready, g + 1)
                    after(act, lg_ready, g)
                    act.activation(h2T[:, :], bank[5][:, :], ACT.Copy).then_inc(h2T_ready, 1)
                act.wait_ge(d_ready, sg + 1)
                act.activation(Ex[:, :, :], L[:, :, :], ACT.Exp)
                act.activation(small["em2"][:, :], small["m2"][:, :], ACT.Exp).then_inc(e_ready, 1)

            modulate(0, 0)
            modulate(0, 1)
            gates(0, 0)
            mixer(0)
            with act.Fori(1, NSG - 1) as sg:
                mixer(sg)
            mixer(NSG - 1, last=True)

            def x_high(it, n):
                act.wait_ge(xT_ready, it * BUFS + (n + 1))
                if not (isinstance(it, int) and n < 2):
                    act.wait_ge(hps_ready, it * (2 * BUFS) + (2 * n - 2))
                act.activation(xh[n % 2][:, :], bank[4 + n % 2][:, 0:TW], ACT.Copy).then_inc(xh_ready, 1)

            def hidden(it, n):
                for e in range(2):
                    act.wait_ge(hps_ready, it * (2 * BUFS) + (2 * n + e + 1))
                    if e == 0:
                        act.wait_ge(bcols_ready, it * BUFS + (n + 1))
                    if not (isinstance(it, int) and n < 1):
                        act.wait_ge(hl_ready, it * (2 * BUFS) + (2 * n - 1 + e))
                    for cc in range(HC):
                        ins = act.activation(hf[e][:, cc, :], bank[2 * e + cc // 2][:, (cc % 2) * TW:(cc % 2 + 1) * TW],
                                             ACT.Relu, bias=bcols[n % 2][:, e * HC + cc:e * HC + cc + 1])
                    ins.then_inc(hf_ready, 1)

            def y_low(it, n):
                act.wait_ge(yps_ready, it * BUFS + (n + 1))
                if not (isinstance(it, int) and n < 1):
                    act.wait_ge(ysb_ready, it * BUFS + n)
                for t in range(HALVES):
                    ins = act.activation(ylo[:, t, :], bank[6 + t][:, 0:D], ACT.Copy, scale=meta[n % BUFS][:, t, 0:1])
                ins.then_inc(ylo_ready, 1)

            act.wait_ge(table_ready, 1)
            turns = loop_turns(act)
            x_high(0, 0)
            for n in range(BUFS):
                x_high(0, n + 1)
                hidden(0, n)
                if n:
                    y_low(0, n - 1)
            with act.Fori(1, turns) as it:
                for k in range(BUFS):
                    x_high(it, k + 1)
                    hidden(it, k)
                    y_low(it, k - 1)
            y_low(last_turn(act), BUFS - 1)
            def store(sg):
                for q in range(NQ):
                    act.wait_ge(yout_ready, sg * NQ + q + 1)
                    act.dma_start(out_t[:, bass.ds(sg * SGT + q * GT, GT), :], yout[q][:, :, :]).then_inc(stored[q], 16)

            store(0)
            with act.Fori(1, NSG) as sg:
                store(sg)
            for q in range(NQ):
                act.wait_ge(stored[q], 16 * NSG)

        @block.vector
        def _(dve):
            base, steps = 0, 0

            def mark(ins):
                nonlocal steps
                ins.then_inc(dve_step, 1)
                steps += 1

            def join():
                dve.wait_ge(dve_step, base + steps)

            def step(ins):
                mark(ins)
                join()

            def signed_clamp(dst, sg_t, ab_t, src):
                step(dve.tensor_copy(dst, src))
                mark(dve.tensor_scalar(sg_t, dst, 0.0, 2.0, ALU.is_ge, ALU.mult))
                step(dve.tensor_scalar(ab_t, dst, -1.0, 0.25, ALU.mult, ALU.max))
                step(dve.tensor_tensor(ab_t, ab_t, dst, ALU.max))
                return dve.scalar_tensor_tensor(out=dst, in0=sg_t, scalar=1.0, in1=ab_t, op0=ALU.subtract, op1=ALU.mult)

            def variances(st, n):
                m0, M0, m1, M1 = (st[:, 0:n, i] for i in (1, 2, 4, 5))
                mark(dve.tensor_tensor(lnt[:, 0, 0:n], m0, m1, ALU.add))
                mark(dve.tensor_tensor(lnt[:, 1, 0:n], m0, m1, ALU.subtract))
                step(dve.tensor_tensor(lnt[:, 2, 0:n], M0, M1, ALU.add))
                step(dve.tensor_tensor(lnt[:, 1, 0:n], lnt[:, 1, 0:n], lnt[:, 1, 0:n], ALU.mult))
                return dve.scalar_tensor_tensor(out=lnt[:, 3, 0:n], in0=lnt[:, 1, 0:n], scalar=D / 4.0,
                                                in1=lnt[:, 2, 0:n], op0=ALU.mult, op1=ALU.add)

            def scales(std, rstd, nmr, n):
                step(dve.reciprocal(rstd[:, 0:n], std[:, 0:n]))
                step(dve.scalar_tensor_tensor(out=nmr[:, 0:n], in0=lnt[:, 0, 0:n], scalar=-0.5, in1=rstd[:, 0:n],
                                              op0=ALU.mult, op1=ALU.mult))

            dve.wait_ge(consts_in, 16 * N_CONST)
            dve.wait_ge(iota_done, 1)
            mark(dve.tensor_scalar(bhalf[:, :], bcol[:, 0:2], 0.5, None, ALU.mult))
            dve.wait_ge(setup_act, 1)
            step(dve.scalar_tensor_tensor(out=csilu[:, :], in0=ctanh[:, :], scalar=1.0, in1=csb[:, :],
                                          op0=ALU.add, op1=ALU.mult))
            dve.tensor_scalar(csilu[:, :], csilu[:, :], 0.5, None, ALU.mult).then_inc(setup_dve, 1)
            dve.wait_ge(setup_pe, 1)
            dve.tensor_copy(csT[:, :], bank[0][:, 0:B]).then_inc(setup_dve, 1)
            dve.wait_ge(setup_pe, 2)
            dve.tensor_copy(wT[:, :, :], bank[1][:, 0:3 * D].rearrange("p (m d) -> p m d", m=3))
            mark(dve.tensor_copy(b1col[:, :], bank[2][:, 2 * E:2 * E + E * HC]))
            dve.tensor_copy(gwT[:, :], bank[2][:, 0:E]).then_inc(setup_dve, 1)
            dve.wait_ge(setup_pe, 3)
            mark(dve.tensor_copy(sa[:, :], bank[3][:, 0:B]))
            mark(dve.tensor_scalar(ca1[:, :], bank[3][:, B:2 * B], 1.0, None, ALU.add))
            step(signed_clamp(gaN[:, :], gasg[:, :], gaab[:, :], bank[3][:, 2 * B:3 * B]))
            step(dve.tensor_scalar(gaN[:, :], gaN[:, :], -0.5, None, ALU.mult))
            dve.tensor_scalar(gabv[:, :], gaN[:, :], bcol[:, 2:3], None, ALU.mult).then_inc(setup_dve, 1)
            dve.tensor_copy(modr[:, 0, :], bank[4][0:B, 0:D])
            dve.tensor_scalar(modr[:, 1, :], bank[4][0:B, D:2 * D], 1.0, None, ALU.add)
            signed_clamp(modr[:, 2, :], gbsg[:, :], gbab[:, :], bank[4][0:B, 2 * D:3 * D]).then_inc(setup_dve, 1)
            b2v = [b2row[row:row + 1, :].rearrange("p (e h) -> p e h", e=E)[:, :, 0:D] for row in (0, 32)]
            b2f = bstage[:, :].rearrange("p (e d) -> p e d", e=E)
            step(dve.tensor_copy(b2v[0], b2f))
            mark(dve.tensor_tensor(b2v[1], b2f, b2v[0], ALU.subtract))
            for s in range(NSG):
                dve.wait_ge(x_in[s], 16)
                with dve.Fori(0, SGT // GT) as t4:
                    for k in range(GT):
                        t = t4 * GT + (s * SGT + k)
                        dve.bn_stats(st1[:, bass.ds(t, 1), :].rearrange("p o s -> p (o s)"),
                                     xs[:, bass.ds(t, 1), :].rearrange("p o d -> p (o d)")).then_inc(dve_step, 1)
                steps += SGT
            join()
            variances(st1, NT).then_inc(v1_ready, 1)
            dve.wait_ge(std1_ready, 1)
            scales(std1, rstd1, nmr1, NT)

            steps_per_sg = 50
            m = {n: t[:, :] for n, t in small.items()}

            def wide(t2, n):
                return t2.unsqueeze(2).to_broadcast([P, SGT, n])

            def over_tiles(t2, n):
                return t2.unsqueeze(1).to_broadcast([P, SGT, n])

            def normalize(sg, q):
                after(dve, xnT_ready, sg * NQ + (q - 1))
                for j in range(GT):
                    t = sg * SGT + (q * GT + j)
                    ins = dve.tensor_scalar(xn[q % 2][:, j * P:(j + 1) * P],
                                            xs[:, bass.ds(t, 1), :].rearrange("p o d -> p (o d)"),
                                            rstd1[:, bass.ds(t, 1)], nmr1[:, bass.ds(t, 1)], ALU.mult, ALU.add)
                ins.then_inc(xn_ready, 1)

            def scan(sg, q):
                g = sg * NQ + q
                k = q % 2
                dve.wait_ge(gates_ready, g + 1)
                step(dve.scalar_tensor_tensor(out=u[:, :], in0=a[k][:, :], scalar=1.0, in1=vs[k][:, :],
                                              op0=ALU.subtract, op1=ALU.mult))
                for b in range(GB):
                    half = slice(b * S, (b + 1) * S)
                    mark(dve.tensor_tensor_scan(hs[:, half], a[k][:, half], u[:, half], 0.0, ALU.mult, ALU.add))
                join()
                after(dve, rT_ready, g - 1)
                dve.scalar_tensor_tensor(out=r[k][:, :], in0=tg[k][:, :], scalar=1.0, in1=hs[:, :],
                                         op0=ALU.add, op1=ALU.mult).then_inc(r_ready, 1)

            def super_group(sg, last=False):
                nonlocal base, steps
                base, steps = sg * steps_per_sg + start, 0

                def residual(q):
                    dve.wait_ge(rT_ready, sg * NQ + (q + 1))
                    xg = xs[:, bass.ds(sg * SGT + q * GT, GT), :]
                    dve.tensor_tensor(xg, bank[4][:, :].rearrange("p (t d) -> p t d", t=GT), xg,
                                      ALU.add).then_inc(x1_ready, 1)
                    dve.wait_ge(x1_ready, sg * NQ + (q + 1))
                    dve.sem_inc(dve_turn, 1)
                    for j in range(GT):
                        t = sg * SGT + (q * GT + j)
                        ins = dve.bn_stats(st2[:, q * GT + j, :], xs[:, bass.ds(t, 1), :].rearrange("p o d -> p (o d)"))
                    return ins

                for q in range(NQ):
                    if q:
                        scan(sg, q)
                    if not (last and q + 2 >= NQ):
                        normalize(sg, q + 2)
                    if q:
                        residual(q - 1)
                ins = residual(NQ - 1)
                step(ins)
                variances(st2, SGT).then_inc(v2_ready, 1)
                dve.wait_ge(std2_ready, sg + 1)
                scales(std2, rstd2, nmr2, SGT)
                for q in range(NQ):
                    after(dve, scattered[q], sg * (16 * GT))
                    for j in range(q * GT, (q + 1) * GT):
                        ins = dve.tensor_scalar(pay[:, j, 0:D],
                                                xs[:, bass.ds(sg * SGT + j, 1), :].rearrange("p o d -> p (o d)"),
                                                rstd2[:, j:j + 1], nmr2[:, j:j + 1], ALU.mult, ALU.add)
                    ins.then_inc(xn2_ready, 1)
                if not last:
                    scan(sg, NQ)
                dve.wait_ge(lg_ready, sg * NQ + NQ)
                dve.tensor_tensor(L[:, :, :], bank[6][:, 0:SGT * E].rearrange("p (t e) -> p t e", e=E),
                                  over_tiles(gbias[:, :], E), ALU.add).then_inc(L_ready, 1)
                dve.wait_ge(L_ready, sg + 1)
                step(dve.tensor_reduce(m["m1"], L[:, :, :], AX_X, ALU.max))
                step(dve.tensor_tensor(L[:, :, :], L[:, :, :], wide(m["m1"], E), ALU.subtract))
                step(dve.scalar_tensor_tensor(out=cand[:, :, :], in0=L[:, :, :], scalar=0.0,
                                              in1=over_tiles(desc[:, :], E), op0=ALU.is_equal, op1=ALU.mult))
                step(dve.tensor_reduce(m["c1"], cand[:, :, :], AX_X, ALU.max))
                step(dve.tensor_tensor(oh1[:, :, :], over_tiles(desc[:, :], E), wide(m["c1"], E), ALU.is_equal))
                step(dve.scalar_tensor_tensor(out=D2[:, :, :], in0=oh1[:, :, :], scalar=NEG, in1=L[:, :, :],
                                              op0=ALU.mult, op1=ALU.add))
                dve.tensor_reduce(m["m2"], D2[:, :, :], AX_X, ALU.max).then_inc(d_ready, 1)
                dve.wait_ge(d_ready, sg + 1)
                step(dve.tensor_tensor(cand[:, :, :], D2[:, :, :], wide(m["m2"], E), ALU.is_equal))
                step(dve.tensor_tensor(cand[:, :, :], cand[:, :, :], over_tiles(desc[:, :], E), ALU.mult))
                step(dve.tensor_reduce(m["c2"], cand[:, :, :], AX_X, ALU.max))
                mark(dve.tensor_tensor(m["cmax"], m["c1"], m["c2"], ALU.max))
                mark(dve.tensor_tensor(m["cmin"], m["c1"], m["c2"], ALU.min))
                mark(dve.tensor_tensor(m["isl"], m["c1"], m["c2"], ALU.is_gt))
                step(dve.tensor_tensor(m["ish"], m["c1"], m["c2"], ALU.is_lt))
                mark(dve.tensor_scalar(m["elo"], m["cmax"], -1.0, float(E), ALU.mult, ALU.add))
                step(dve.tensor_scalar(m["ehi"], m["cmin"], -1.0, float(E), ALU.mult, ALU.add))
                step(dve.scalar_tensor_tensor(out=m["tri"], in0=m["ehi"], scalar=1.0, in1=m["ehi"],
                                              op0=ALU.subtract, op1=ALU.mult))
                step(dve.scalar_tensor_tensor(out=m["pair"], in0=m["tri"], scalar=0.5, in1=m["elo"],
                                              op0=ALU.mult, op1=ALU.add))
                dve.tensor_tensor(OH[:, :, :], over_tiles(pair_iota[:, :], PAIRS), wide(m["pair"], PAIRS),
                                  ALU.is_equal).then_inc(oh_ready, 1)
                dve.wait_ge(e_ready, sg + 1)
                step(dve.tensor_reduce(m["s"], Ex[:, :, :], AX_X, ALU.add))
                step(dve.reciprocal(m["p1"], m["s"]))
                step(dve.tensor_tensor(m["p2"], m["em2"], m["p1"], ALU.mult))
                mark(dve.tensor_tensor(m["t1"], m["isl"], m["p1"], ALU.mult))
                mark(dve.tensor_tensor(m["t2"], m["ish"], m["p2"], ALU.mult))
                mark(dve.tensor_tensor(m["t3"], m["ish"], m["p1"], ALU.mult))
                step(dve.tensor_tensor(m["t4"], m["isl"], m["p2"], ALU.mult))
                mark(dve.tensor_tensor(pay[:, :, D], m["t1"], m["t2"], ALU.add))
                mark(dve.tensor_tensor(pay[:, :, D + 1], m["t3"], m["t4"], ALU.add))
                mark(dve.tensor_copy(payi[:, :, D + 2], tok[:, bass.ds(sg * SGT, SGT)]))
                dve.wait_ge(oh_ready, sg + 1)
                step(dve.tensor_reduce(seen_add[:, :], OH[:, :, :].rearrange("p t j -> p j t"), AX_X, ALU.add))
                dve.wait_ge(rank_ready, sg + 1)
                mark(dve.tensor_tensor(seen[:, :], seen[:, :], seen_add[:, :], ALU.add))
                step(dve.tensor_tensor(prod[:, :, :], bank[7][:, 0:SGT * PAIRS].rearrange("p (t j) -> p t j", j=PAIRS),
                                       OH[:, :, :], ALU.mult))
                step(dve.tensor_reduce(m["pos"], prod[:, :, :], AX_X, ALU.add))
                dve.scalar_tensor_tensor(out=idx[:, :], in0=m["pair"], scalar=float(STRIDE), in1=m["pos"],
                                         op0=ALU.mult, op1=ALU.add).then_inc(idx_ready, 1)

            normalize(0, 0)
            normalize(0, 1)
            scan(0, 0)
            start = steps
            super_group(0)
            assert steps == steps_per_sg, steps
            with dve.Fori(1, NSG - 1) as sg:
                super_group(sg)
            super_group(NSG - 1, last=True)
            dve.wait_ge(cnt_ready, 1)
            step(dve.tensor_copy(cnt[:, :], bank[6][:, 0:PAIRS]))
            mark(dve.tensor_tensor(padrow[:, :], cnt[0:1, :], region0[0:1, :], ALU.add))
            step(dve.tensor_scalar(cnti[:, :], cnt[:, :], float(TW - 1), None, ALU.add))
            step(dve.tensor_scalar(cntt[:, :], cnti[:, :], TW.bit_length() - 1, None, ALU.arith_shift_right))
            step(dve.tensor_copy(ntl[:, :], cntt[:, :]))
            step(dve.tensor_tensor_scan(tend[:, :], onesf[:, :], ntl[:, :], 0.0, ALU.mult, ALU.add))
            mark(dve.tensor_scalar(le_end[:, :], tend[:, :], pidx[:, 0:1], None, ALU.is_le))
            step(dve.tensor_tensor(tstart[:, :], tend[:, :], ntl[:, :], ALU.subtract))
            step(dve.tensor_scalar(le_start[:, :], tstart[:, :], pidx[:, 0:1], None, ALU.is_le))
            step(dve.tensor_tensor(inpair[:, :], le_start[:, :], le_end[:, :], ALU.subtract))
            mark(dve.scalar_tensor_tensor(out=tt[:, 0, :], in0=tstart[:, :], scalar=pidx[:, 0:1], in1=inpair[:, :],
                                          op0=ALU.subtract, op1=ALU.mult))
            mark(dve.tensor_tensor(tt[:, 1, :], inpair[:, :], elo_of[:, :], ALU.mult))
            step(dve.tensor_tensor(tt[:, 2, :], inpair[:, :], ehi_of[:, :], ALU.mult))
            mark(dve.tensor_reduce(ngone[:, :], le_end[:, :], AX_X, ALU.add))
            step(dve.tensor_scalar(cnti[:, 0:1], tend[:, PAIRS - 1:PAIRS], float(BUFS - 1), None, ALU.add))
            step(dve.tensor_scalar(cntt[:, 0:1], cnti[:, 0:1], 2, None, ALU.arith_shift_right))
            mark(dve.tensor_tensor(tcols[:, 3:4], cntt[:, 0:1], pidx[:, :], ALU.subtract))
            step(dve.tensor_reduce(tcols[:, 0:3], tt[:, :, :], AX_X, ALU.add))
            step(dve.tensor_scalar(base0[:, :], ngone[:, :], float(STRIDE), None, ALU.mult))
            dve.scalar_tensor_tensor(out=tcols[:, 0:1], in0=tcols[:, 0:1], scalar=-float(TW), in1=base0[:, :],
                                     op0=ALU.mult, op1=ALU.add).then_inc(tcols_ready, 1)
            dve.wait_ge(tcolsT_ready, 1)
            dve.tensor_copy(table[:, :], bank[6][0:4, 0:P]).then_inc(table_ready, 1)

            def x_low(it, n):
                k = n % BUFS
                dve.wait_ge(tile_in[k], it * 16 + (n // BUFS * 16 + 16))
                if not (isinstance(it, int) and n < BUFS):
                    dve.wait_ge(ysc[k], (it + n // BUFS) * (16 * HALVES))
                dve.tensor_copy(meta[k][:, :, :], xin[k][:, :, D:ROW]).then_inc(xl_ready, 1)
                dve.wait_ge(xh_ready, it * BUFS + (n + 1))
                dve.tensor_tensor(xl[n % 2][:, :], bank[4 + n % 2][:, 0:TW], xh[n % 2][:, :], ALU.subtract
                                  ).then_inc(xl_ready, 1)

            def biases(it, n):
                for e in range(2):
                    ex = dve.value_load(table[1 + e:2 + e, bass.ds(it * BUFS + n, 1)], min_val=0, max_val=(E - 1) * H)
                    ins = dve.tensor_copy(bcols[n % 2][:, e * HC:(e + 1) * HC], b1col[:, bass.ds(ex // P, HC)])
                ins.then_inc(bcols_ready, 1)

            def split(it, n):
                for e in range(2):
                    dve.wait_ge(hf_ready, it * (2 * BUFS) + (2 * n + e + 1))
                    if not (isinstance(it, int) and n < 2):
                        dve.wait_ge(yps_ready, it * BUFS + (n - 1))
                    dve.tensor_copy(hh[n % 2][e][:, :, :], hf[e][:, :, :]).then_inc(hh_ready, 1)
                    dve.wait_ge(hh_ready, it * (2 * BUFS) + (2 * n + e + 1))
                    dve.tensor_tensor(hl[n % 2][e][:, :, :], hf[e][:, :, :], hh[n % 2][e][:, :, :], ALU.subtract
                                      ).then_inc(hl_ready, 1)

            def y_sum(it, n):
                k = n % BUFS
                dve.wait_ge(ylo_ready, it * BUFS + (n + 1))
                for t in range(HALVES):
                    ins = dve.scalar_tensor_tensor(out=ysb[k][:, t, :], in0=bank[6 + t][:, D:2 * D],
                                                   scalar=meta[k][:, t, 1:2], in1=ylo[:, t, :],
                                                   op0=ALU.mult, op1=ALU.add)
                ins.then_inc(ysb_ready, 1)

            dve.wait_ge(table_ready, 1)
            turns = loop_turns(dve)
            biases(0, 0)
            x_low(0, 0)
            for n in range(BUFS):
                x_low(0, n + 1)
                biases(0, n + 1)
                split(0, n)
                if n:
                    y_sum(0, n - 1)
            with dve.Fori(1, turns) as it:
                for k in range(BUFS):
                    x_low(it, k + 1)
                    biases(it, k + 1)
                    split(it, k)
                    y_sum(it, k - 1)
            y_sum(last_turn(dve), BUFS - 1)
            def combine(sg):
                for q in range(NQ):
                    dve.wait_ge(ymul_ready, sg * NQ + q + 1)
                    after(dve, stored[q], sg * 16)
                    dve.tensor_tensor(yout[q][:, :, :], yin[q][:, :, :], xs[:, bass.ds(sg * SGT + q * GT, GT), :],
                                      ALU.add).then_inc(yout_ready, 1)

            combine(0)
            with dve.Fori(1, NSG) as sg:
                combine(sg)

        @block.tensor
        def _(pe):
            pe.wait_ge(consts_in, 16 * N_CONST)
            pe.wait_ge(iota_done, 1)
            pe.wait_ge(setup_dve, 1)
            pe.transpose(bank[0][:, 0:B], csilu[:, :], ident[0:B, 0:B]).then_inc(setup_pe, 1)
            for i in range(3):
                pe.transpose(bank[1][:, i * D:(i + 1) * D], wraw[:, i, :], ident[:, :])
            pe.transpose(bank[2][:, 2 * E:2 * E + E * HC], b1c[:, :], ident[0:E * HC, 0:E * HC])
            pe.transpose(bank[2][:, 0:E], gw[:, :], ident[0:E, 0:E]).then_inc(setup_pe, 1)
            pe.wait_ge(setup_dve, 2)
            for i in range(3):
                pe.matmul(bank[3][:, i * B:(i + 1) * B], wmods[:, i * D:(i + 1) * D], csT[:, :], start=True, stop=True)
            pe.matmul(bank[4][0:B, 0:3 * D], csT[:, :], wmods[:, 3 * D:6 * D], start=True, stop=True).then_inc(setup_pe, 1)
            pe.wait_ge(setup_dve, 3)

            def turn_xn(sg, q):
                pe.wait_ge(xn_ready, sg * NQ + (q + 1))
                after(pe, hT_ready, sg * NQ + q)
                for j in range(GT):
                    ins = pe.transpose(bank[0][:, j * P:(j + 1) * P], xn[q % 2][:, j * P:(j + 1) * P], ident[:, :])
                ins.then_inc(xnT_ready, 1)

            def project(sg, q):
                g = sg * NQ + q
                pe.wait_ge(hT_ready, g + 1)
                after(pe, z_used, g)
                for i in (1, 2, 0):
                    ins = pe.matmul(bank[1 + i][:, :], wT[:, i, :], hT[q % 2][:, :], start=True, stop=True)
                ins.then_inc(z_ready, 1)

            def super_group(sg, last=False):
                def turn_r(q):
                    pe.wait_ge(r_ready, sg * NQ + (q + 1))
                    after(pe, x1_ready, sg * NQ + q)
                    for j in range(GT):
                        ins = pe.transpose(bank[4][:, j * P:(j + 1) * P], r[q % 2][:, j * P:(j + 1) * P], ident[:, :])
                    ins.then_inc(rT_ready, 1)

                for q in range(1, NQ):
                    if not (last and q + 1 == NQ):
                        turn_xn(sg, q + 1)
                    project(sg, q)
                    turn_r(q - 1)
                turn_r(NQ - 1)
                if not last:
                    turn_xn(sg, NQ + 1)
                    project(sg, NQ)
                after(pe, L_ready, sg)
                for q in range(NQ):
                    g = sg * NQ + q
                    pe.wait_ge(h2_ready, g + 1)
                    after(pe, h2T_ready, g)
                    for j in range(GT):
                        ins = pe.transpose(bank[5][:, j * P:(j + 1) * P], pay[:, q * GT + j, 0:D], ident[:, :])
                    ins.then_inc(h2Tp_ready, 1)
                    pe.wait_ge(h2T_ready, g + 1)
                    for j in range(GT):
                        o = (q * GT + j) * E
                        ins = pe.matmul(bank[6][:, o:o + E], h2T[:, j * P:(j + 1) * P], gwT[:, :], start=True, stop=True)
                    ins.then_inc(lg_ready, 1)
                pe.wait_ge(oh_ready, sg + 1)
                after(pe, idx_ready, sg)
                ohf = OH[:, :, :].rearrange("p t j -> p (t j)")
                rank = bank[7][:, 0:SGT * PAIRS]
                pe.matmul(rank, upper[:, :], ohf, start=True, stop=False)
                for t in range(1, SGT):
                    pe.matmul(rank[:, t * PAIRS:], ones_bf[:, :], ohf[:, 0:(SGT - t) * PAIRS], start=False, stop=False)
                pe.matmul(rank.rearrange("p (t j) -> p t j", j=PAIRS), ones_bf[:, :],
                          seen[:, :].unsqueeze(1).to_broadcast([P, SGT, PAIRS]), start=False, stop=True
                          ).then_inc(rank_ready, 1)

            turn_xn(0, 0)
            turn_xn(0, 1)
            project(0, 0)
            super_group(0)
            with pe.Fori(1, NSG - 1) as sg:
                super_group(sg)
            super_group(NSG - 1, last=True)
            pe.wait_ge(idx_ready, NSG)
            pe.matmul(bank[6][:, 0:PAIRS], ones_bf[:, :], seen[:, :], start=True, stop=True).then_inc(cnt_ready, 1)
            pe.wait_ge(tcols_ready, 1)
            pe.transpose(bank[6][0:4, 0:P], tcols[:, :], ident[:, :]).then_inc(tcolsT_ready, 1)
            pe.wait_ge(table_ready, 1)
            pe.wait_ge(w_lo, 2)

            def turn(it, n):
                pe.wait_ge(tile_in[n % BUFS], it * 16 + (n // BUFS * 16 + 16))
                for t in range(HALVES):
                    ins = pe.transpose(bank[4 + n % 2][:, t * P:(t + 1) * P], xin[n % BUFS][:, t, 0:D], ident[:, :])
                ins.then_inc(xT_ready, 1)

            def experts_of(it, n):
                return [pe.value_load(table[1 + e:2 + e, bass.ds(it * BUFS + n, 1)], min_val=0, max_val=(E - 1) * H)
                        for e in range(2)]

            def layer1(it, n, ex):
                pe.wait_ge(xl_ready, it * (2 * BUFS) + (2 * n + 2))
                for e in range(2):
                    if not (isinstance(it, int) and n < 1):
                        pe.wait_ge(hf_ready, it * (2 * BUFS) + (2 * n - 1 + e))
                    for cc in range(HC):
                        o = bank[2 * e + cc // 2][:, (cc % 2) * TW:(cc % 2 + 1) * TW]
                        whi, wlo = (w[:, bass.ds(ex[e] + cc * P, P)] for w in (w1hi, w1lo))
                        pe.matmul(o, whi, xh[n % 2][:, :], start=True, stop=False)
                        pe.matmul(o, whi, xl[n % 2][:, :], start=False, stop=False)
                        ins = pe.matmul(o, wlo, xh[n % 2][:, :], start=False, stop=True)
                    ins.then_inc(hps_ready, 1)

            def layer2(it, n, ex):
                if not (isinstance(it, int) and n < 1):
                    pe.wait_ge(ysb_ready, it * BUFS + n)
                pe.wait_ge(hl_ready, it * (2 * BUFS) + (2 * n + 2))
                for e in range(2):
                    o = [bank[6 + t][:, e * D:(e + 1) * D] for t in range(HALVES)]
                    bias = b2row[:, bass.ds(ex[e], D)]
                    for t in range(HALVES):
                        pe.matmul(o[t], ones16[:, :], bias, start=True, stop=False)
                    for cc in range(HC):
                        whi, wlo = (w[:, bass.ds(ex[e] + cc * D, D)] for w in (w2hi, w2lo))
                        for t in range(HALVES):
                            pe.matmul(o[t], hh[n % 2][e][:, cc, t * P:(t + 1) * P], whi, start=False, stop=False)
                            pe.matmul(o[t], hl[n % 2][e][:, cc, t * P:(t + 1) * P], whi, start=False, stop=False)
                        for t in range(HALVES):
                            ins = pe.matmul(o[t], hh[n % 2][e][:, cc, t * P:(t + 1) * P], wlo, start=False,
                                            stop=(cc == HC - 1))
                ins.then_inc(yps_ready, 1)

            turns = loop_turns(pe)
            turn(0, 0)
            for n in range(BUFS):
                now = experts_of(0, n)
                turn(0, n + 1)
                layer1(0, n, now)
                if n:
                    layer2(0, n - 1, before)
                before = now
            with pe.Fori(1, turns) as it:
                before = experts_of(it, -1)
                for k in range(BUFS):
                    now = experts_of(it, k)
                    turn(it, k + 1)
                    layer1(it, k, now)
                    layer2(it, k - 1, before)
                    before = now
            last = last_turn(pe)
            layer2(last, BUFS - 1, experts_of(last, BUFS - 1))


_INS = ["L0_attn_x", "L0_attn_Wg", "L0_attn_bg", "L0_attn_Wv", "L0_attn_bv", "L0_attn_Wd", "L0_attn_bd",
        "L0_ffn_gate_w", "L0_ffn_gate_b", "L0_ffn_w1", "L0_ffn_b1", "L0_ffn_w2", "L0_ffn_b2", "L0_c", "L0_wmod"]
_OUTS = [((B, S, D), "float32")]


def kernel(**inputs):
    import numpy as _np
    import concourse.bacc as _bacc
    from concourse import mybir as _mybir
    from concourse.bass_utils import run_bass_kernel_spmd as _run

    nc = _bacc.Bacc("TRN2", target_bir_lowering=False, num_devices=1)
    arrays, args = {}, []
    for name in _INS:
        arr = _np.ascontiguousarray(inputs[name])
        arrays[f"in_{name}_dram"] = arr
        args.append(nc.dram_tensor(f"in_{name}_dram", arr.shape, _mybir.dt.from_np(arr.dtype),
                                   kind="ExternalInput").ap())
    for i, (shape, dtype) in enumerate(_OUTS):
        dt = _mybir.dt.from_np(_np.dtype(dtype))
        args.append(nc.dram_tensor(f"out_{i}_dram", shape, dt, kind="ExternalOutput").ap())
    adaln_moe_kernel(nc, *args)
    res = _run(nc, [arrays], core_ids=[0])
    got = tuple(res.results[0][f"out_{i}_dram"] for i in range(len(_OUTS)))
    return got[0]
```
